# Optimizing a Trainium2 kernel written in Bass

```python
import numpy as np
import jax
import jax.numpy as jnp

def _softmax(x, axis=-1):
    return jax.nn.softmax(x, axis=axis)

def _gelu(x):
    return jax.nn.gelu(x, approximate=True)

def _silu(x):
    return jax.nn.silu(x)

def _sigmoid(x):
    return jax.nn.sigmoid(x)

def _layernorm(x, axis=-1, eps=1e-05):
    m = jnp.mean(x, axis=axis, keepdims=True)
    v = jnp.var(x, axis=axis, keepdims=True)
    return (x - m) / jnp.sqrt(v + eps)

def _scatter_add(tgt, idx, src, axis=0):
    return tgt.at[idx].add(src)

def _segment_sum(src, seg, n):
    return jax.ops.segment_sum(src, seg, n)
kernel_name = 'mk_adj_preln_d2_adj_r2_ba2aaf'

def setup_inputs(seed: int=0):
    np.random.seed(seed)
    _w = jnp.asarray

    def _rec_inputs():
        import jax
        import jax.numpy as jnp
        _gk = jax.random.key(seed)
        x = -0.0002928 + 1 * jax.random.normal(jax.random.fold_in(_gk, 1), (32, 256, 128), jnp.float32)
        _w = (1.0 + jnp.arange(256, dtype=jnp.float32)) ** (-0.5)
        _w = _w / _w.mean()
        _pij = jnp.clip(0.03125 * _w[:, None] * _w[None, :], 0.0, 1.0)
        _a = jax.random.uniform(jax.random.fold_in(_gk, 2), (32, 256, 256)) < _pij
        _af = _a.astype(jnp.float32)
        adj = _af
        return (x, adj)
    x, adj = _rec_inputs()

    def _L0_gnn_setup():
        import jax, jax.numpy as jnp
        import numpy as np
        ALPHA = 0.2
        NEG = -9000000000000000.0
        key = jax.random.key(seed)
        k1, k2, k3, k4 = jax.random.split(key, 4)
        B, N, F_in, F_out = (8, 1024, 128, 128)
        x = jax.random.normal(k1, (B, N, F_in), dtype=jnp.float32)
        adj = (jax.random.uniform(k2, (B, N, N)) < 0.05).astype(jnp.float32)
        W = jax.random.normal(k3, (F_in, F_out), jnp.float32) * (1.414 * np.sqrt(2.0 / (F_in + F_out)))
        a = jax.random.normal(k4, (2 * F_out, 1), jnp.float32) * (1.414 * np.sqrt(2.0 / (2 * F_out + 1)))
        return {'input': x, 'adj': adj, 'W': W, 'a': a}
    _L0_gnn_all = _L0_gnn_setup()
    _L0_gnn_in = {k: v for k, v in _L0_gnn_all.items() if k in ('W', 'a')}
    del _L0_gnn_all

    def _L1_gnn_setup():
        import jax, jax.numpy as jnp
        import numpy as np
        from jax import lax
        DIM = 128
        EPS = 1e-05

        def _bn(h, g, b, m, v):
            scale = g / jnp.sqrt(v + EPS)
            return h * scale[None, :, None] + (b - m * scale)[None, :, None]

        def _conv1d(h, w, pad):
            return lax.conv_general_dilated(h, w, window_strides=(1,), padding=[(pad, pad)], dimension_numbers=('NCH', 'OIH', 'NCH'))
        key = jax.random.key(seed)
        ks = jax.random.split(key, 16)
        bs, n, d = (16, 1024, DIM)
        s = 0.05
        return {'x': jax.random.normal(ks[0], (bs, n, d), jnp.float32), 'mask': jnp.ones((bs, n, n), jnp.float32), 'w_se': jax.random.normal(ks[1], (3, d), jnp.float32) * s, 'b_se': jnp.zeros((3,), jnp.float32), 'conv1_w': jax.random.normal(ks[2], (d, d, 1), jnp.float32) * s, 'bn1_g': jnp.ones((d,), jnp.float32), 'bn1_b': jnp.zeros((d,), jnp.float32), 'bn1_m': jnp.zeros((d,), jnp.float32), 'bn1_v': jnp.ones((d,), jnp.float32), 'conv2_w': jax.random.normal(ks[3], (d, d, 17), jnp.float32) * s, 'bn2_g': jnp.ones((d,), jnp.float32), 'bn2_b': jnp.zeros((d,), jnp.float32), 'bn2_m': jnp.zeros((d,), jnp.float32), 'bn2_v': jnp.ones((d,), jnp.float32), 'w_msg': jax.random.normal(ks[4], (d, d), jnp.float32) * s, 'b_msg': jnp.zeros((d,), jnp.float32), 'w_ih': jax.random.normal(ks[5], (3 * d, 2 * d), jnp.float32) * s, 'b_ih': jnp.zeros((3 * d,), jnp.float32), 'w_hh': jax.random.normal(ks[6], (3 * d, d), jnp.float32) * s, 'b_hh': jnp.zeros((3 * d,), jnp.float32)}
    _L1_gnn_all = _L1_gnn_setup()
    _L1_gnn_in = {k: v for k, v in _L1_gnn_all.items() if k in ('w_se', 'b_se', 'conv1_w', 'bn1_g', 'bn1_b', 'bn1_m', 'bn1_v', 'conv2_w', 'bn2_g', 'bn2_b', 'bn2_m', 'bn2_v', 'w_msg', 'b_msg', 'w_ih', 'b_ih', 'w_hh', 'b_hh')}
    del _L1_gnn_all
    return {'x': x, 'adj': adj, 'L0_gnn_W': _L0_gnn_in['W'], 'L0_gnn_a': _L0_gnn_in['a'], 'L1_gnn_w_se': _L1_gnn_in['w_se'], 'L1_gnn_b_se': _L1_gnn_in['b_se'], 'L1_gnn_conv1_w': _L1_gnn_in['conv1_w'], 'L1_gnn_bn1_g': _L1_gnn_in['bn1_g'], 'L1_gnn_bn1_b': _L1_gnn_in['bn1_b'], 'L1_gnn_bn1_m': _L1_gnn_in['bn1_m'], 'L1_gnn_bn1_v': _L1_gnn_in['bn1_v'], 'L1_gnn_conv2_w': _L1_gnn_in['conv2_w'], 'L1_gnn_bn2_g': _L1_gnn_in['bn2_g'], 'L1_gnn_bn2_b': _L1_gnn_in['bn2_b'], 'L1_gnn_bn2_m': _L1_gnn_in['bn2_m'], 'L1_gnn_bn2_v': _L1_gnn_in['bn2_v'], 'L1_gnn_w_msg': _L1_gnn_in['w_msg'], 'L1_gnn_b_msg': _L1_gnn_in['b_msg'], 'L1_gnn_w_ih': _L1_gnn_in['w_ih'], 'L1_gnn_b_ih': _L1_gnn_in['b_ih'], 'L1_gnn_w_hh': _L1_gnn_in['w_hh'], 'L1_gnn_b_hh': _L1_gnn_in['b_hh']}

def reference(x, adj, L0_gnn_W, L0_gnn_a, L1_gnn_w_se, L1_gnn_b_se, L1_gnn_conv1_w, L1_gnn_bn1_g, L1_gnn_bn1_b, L1_gnn_bn1_m, L1_gnn_bn1_v, L1_gnn_conv2_w, L1_gnn_bn2_g, L1_gnn_bn2_b, L1_gnn_bn2_m, L1_gnn_bn2_v, L1_gnn_w_msg, L1_gnn_b_msg, L1_gnn_w_ih, L1_gnn_b_ih, L1_gnn_w_hh, L1_gnn_b_hh):
    import jax
    import jax.numpy as jnp

    def _L0_gnn_ref(input, adj, W, a):
        import jax, jax.numpy as jnp
        import numpy as np
        ALPHA = 0.2
        NEG = -9000000000000000.0
        F_out = W.shape[1]
        h = input @ W
        a1 = a[:F_out, 0]
        a2 = a[F_out:, 0]
        s = jnp.einsum('bnf,f->bn', h, a1 + a2)
        e = jax.nn.leaky_relu(s, ALPHA)[:, :, None]
        logits = jnp.where(adj > 0, e, NEG)
        att = jax.nn.softmax(logits, axis=2)
        h_prime = jnp.einsum('bij,bjf->bif', att, h)
        return jax.nn.elu(h_prime)

    def _L1_gnn_ref(x, mask, w_se, b_se, conv1_w, bn1_g, bn1_b, bn1_m, bn1_v, conv2_w, bn2_g, bn2_b, bn2_m, bn2_v, w_msg, b_msg, w_ih, b_ih, w_hh, b_hh):
        import jax, jax.numpy as jnp
        import numpy as np
        from jax import lax
        DIM = 128
        EPS = 1e-05

        def _bn(h, g, b, m, v):
            scale = g / jnp.sqrt(v + EPS)
            return h * scale[None, :, None] + (b - m * scale)[None, :, None]

        def _conv1d(h, w, pad):
            return lax.conv_general_dilated(h, w, window_strides=(1,), padding=[(pad, pad)], dimension_numbers=('NCH', 'OIH', 'NCH'))
        d = x.shape[-1]
        xc = jnp.transpose(x, (0, 2, 1))
        h = _bn(_conv1d(xc, conv1_w, 0), bn1_g, bn1_b, bn1_m, bn1_v)
        h = jax.nn.relu(h)
        h = _bn(_conv1d(h, conv2_w, 8), bn2_g, bn2_b, bn2_m, bn2_v)
        x_conv = jnp.transpose(jax.nn.relu(h + xc), (0, 2, 1))
        s = x @ w_se.T + b_se
        sq = jnp.sum(s * s, axis=-1)
        dist = sq[:, :, None] + sq[:, None, :] - 2.0 * jnp.einsum('bnd,bmd->bnm', s, s)
        A = jnp.exp(-dist) * mask
        msg = jax.nn.relu(x @ w_msg.T + b_msg)
        x_nmp = jnp.einsum('bnm,bmd->bnd', A, msg)
        x_in = jnp.concatenate([x_conv, x_nmp], axis=-1)
        gi = x_in @ w_ih.T + b_ih
        gh = x @ w_hh.T + b_hh
        gi_r, gi_z, gi_n = (gi[..., :d], gi[..., d:2 * d], gi[..., 2 * d:])
        gh_r, gh_z, gh_n = (gh[..., :d], gh[..., d:2 * d], gh[..., 2 * d:])
        r = jax.nn.sigmoid(gi_r + gh_r)
        z = jax.nn.sigmoid(gi_z + gh_z)
        nn_ = jnp.tanh(gi_n + r * gh_n)
        return (1.0 - z) * nn_ + z * x
    h = jnp.maximum(_layernorm(x, axis=-1), 0.0)
    x = x + _L0_gnn_ref(h, adj, L0_gnn_W, L0_gnn_a)
    h = jnp.maximum(_layernorm(x, axis=-1), 0.0)
    x = x + _L1_gnn_ref(h, adj, L1_gnn_w_se, L1_gnn_b_se, L1_gnn_conv1_w, L1_gnn_bn1_g, L1_gnn_bn1_b, L1_gnn_bn1_m, L1_gnn_bn1_v, L1_gnn_conv2_w, L1_gnn_bn2_g, L1_gnn_bn2_b, L1_gnn_bn2_m, L1_gnn_bn2_v, L1_gnn_w_msg, L1_gnn_b_msg, L1_gnn_w_ih, L1_gnn_b_ih, L1_gnn_w_hh, L1_gnn_b_hh)
    return x

_drawn_inputs = setup_inputs


def setup_inputs(seed=0):
    import zlib

    import numpy as np

    out = dict(_drawn_inputs(seed))
    spreads = {'L1_gnn_b_se': (0.0, 0.8),
     'L1_gnn_bn1_g': (1.0, 0.6),
     'L1_gnn_bn1_b': (0.0, 0.362),
     'L1_gnn_bn1_m': (0.0, 0.349),
     'L1_gnn_bn1_v': (1.0, 0.6),
     'L1_gnn_bn2_g': (1.0, 0.6),
     'L1_gnn_bn2_b': (0.0, 0.677),
     'L1_gnn_bn2_m': (0.0, 0.56),
     'L1_gnn_bn2_v': (1.0, 0.6),
     'L1_gnn_b_msg': (0.0, 0.1),
     'L1_gnn_b_ih': (0.0, 0.274),
     'L1_gnn_b_hh': (0.0, 0.439)}
    factors = {}
    for name, (base, spread) in spreads.items():
        noise = np.random.default_rng([zlib.crc32(name.encode()), seed]).standard_normal(out[name].shape)
        drawn = base * np.exp(spread * noise) if base else spread * noise
        out[name] = jnp.asarray(drawn.astype(out[name].dtype))
    for name, factor in factors.items():
        out[name] = (out[name] * factor).astype(out[name].dtype)
    return out
```

```python
import numpy as np
import concourse.bass as bass
from concourse import mybir
from contextlib import ExitStack

F32 = mybir.dt.float32
F32R = mybir.dt.float32r
BF16 = mybir.dt.bfloat16
I32 = mybir.dt.int32
ALU = mybir.AluOpType
ACT = mybir.ActivationFunctionType

B, N, D = 32, 256, 128
PAIRS = B // 2
TAPS = 17
PAD = TAPS // 2
GATES = 3
S3 = 3
EPS = 1e-5
NEG = -9000000000000000.0
ALPHA = 0.2
RSQRT_SEED = 1597463007.0
FIRST_STEP, LAST_STEP = -2, PAIRS
LOOP_FROM, LOOP_TO = 2, PAIRS - 2


def bass_gnn_kernel(nc, x, adj, W, a, w_se, b_se, conv1_w, bn1_g, bn1_b, bn1_m, bn1_v, conv2_w,
                    bn2_g, bn2_b, bn2_m, bn2_v, w_msg, b_msg, w_ih, b_ih, w_hh, b_hh, out):
    x_v = x.rearrange("(t b) (p h) f -> t p b (h f)", b=2, h=2)
    adj_v = adj.rearrange("(t b) (p h) j -> t p b (h j)", b=2, h=2)
    out_v = out.rearrange("(t b) (p h) f -> t p b (h f)", b=2, h=2)

    ROWS = [(w_se, 3), (bn1_g, 1), (bn1_b, 1), (bn1_m, 1), (bn1_v, 1), (bn2_g, 1), (bn2_b, 1),
            (bn2_m, 1), (bn2_v, 1), (b_ih, 3), (b_hh, 3), (a, 2)]
    C_SE, C_BN1, C_BN2, C_IH, C_HH, C_A = 0, 3, 7, 11, 14, 17
    NPARAM = 8

    with ExitStack() as ctx:
        def sb(name, shape, dt=F32):
            return ctx.enter_context(nc.sbuf_tensor(name, shape, dt))

        def sem(name):
            return ctx.enter_context(nc.semaphore(name))

        ident = sb("ident", [128, 128])
        ident_b = sb("ident_b", [128, 128], BF16)
        rows = sb("rows", [32, 128])
        cols = sb("cols", [128, 32])
        W_sb = sb("W_sb", [128, 128])
        WT = sb("WT", [128, 128])
        conv1_raw = sb("conv1_raw", [128, 128])
        msg_raw = sb("msg_raw", [128, 128])
        ih_raw = sb("ih_raw", [128, GATES, 2 * D])
        hh_raw = sb("hh_raw", [128, GATES, D])
        conv2_raw = sb("conv2_raw", [128, D * TAPS])
        w1T = sb("w1T", [128, 128])
        w_ms = sb("w_ms", [128, 132])
        ihT = sb("ihT", [128, GATES * 2, 128])
        hhT = sb("hhT", [128, GATES, 128])
        w2H = sb("w2H", [128, TAPS, 128], F32R)
        w2L = sb("w2L", [128, TAPS, 128], F32R)
        b_ms = sb("b_ms", [128, 132])
        a_bc = sb("a_bc", [128, 128])
        wa = sb("wa", [128, 128])
        bnv = sb("bnv", [128, 2])
        bnr = sb("bnr", [128, 2])
        bnt = sb("bnt", [128, 2])
        bnscale = sb("bnscale", [128, 2])
        bnbias = sb("bnbias", [128, 2])
        gate_b = sb("gate_b", [128, 4])
        asum = sb("asum", [128, 1])

        zeros = sb("zeros", [128, 4])
        three_halves = sb("three_halves", [128, 4])

        x_sb = sb("x_sb", [128, 2, 4, D])
        adj_sb = sb("adj_sb", [128, 2, 4, N])
        st0 = sb("st0", [128, 4, 6])
        mv0 = sb("mv0", [128, 4, 2])
        var0 = sb("var0", [128, 4])
        nhvar0 = sb("nhvar0", [128, 4])
        seed0 = sb("seed0", [128, 4])
        rstd0 = sb("rstd0", [128, 4])
        nt0 = sb("nt0", [128, 4])
        g0 = sb("g0", [128, 4, D])
        h0H = sb("h0H", [128, 4, D], F32R)
        h0L = sb("h0L", [128, 4, D], F32R)
        junk = sb("junk", [128, 4, D])
        mask = sb("mask", [128, 4, N], BF16)
        numer = sb("numer", [128, 4, N], BF16)
        deg = sb("deg", [128, 4])
        srow = sb("srow", [128, 4])
        erow = sb("erow", [128, 4])
        some = sb("some", [128, 2, 4])
        fill = sb("fill", [128, 2, 4])
        cand = sb("cand", [128, 2, 4])
        rmax = sb("rmax", [128, 4])
        sraw = sb("sraw", [128, 2, 4])
        sdiff = sb("sdiff", [128, 2, 4])
        pexp = sb("pexp", [128, 2, 4])
        pdiff = sb("pdiff", [128, 4])
        dsum = sb("dsum", [128, 4])
        den = sb("den", [128, 4])
        rden = sb("rden", [128, 2, 4])

        maskT = sb("maskT", [128, 2, 2, 2 * D], F32R)
        zT = sb("zT", [128, 4, D])
        y = sb("y", [128, 4 * D])
        yneg = sb("yneg", [128, 4 * D])
        yexp = sb("yexp", [128, 4 * D])
        ysum = sb("ysum", [128, 4 * D])
        x1 = sb("x1", [128, 2, 4, D])
        st1 = sb("st1", [128, 4, 6])
        mv1 = sb("mv1", [128, 4, 2])
        var1 = sb("var1", [128, 4])
        nhvar1 = sb("nhvar1", [128, 4])
        seed1 = sb("seed1", [128, 4])
        rstd1 = sb("rstd1", [128, 4])
        nt1 = sb("nt1", [128, 4])
        g1 = sb("g1", [128, 4, D])
        h1 = sb("h1", [128, 4, D])
        hT = sb("hT", [128, 2, 2 * N])
        c1 = sb("c1", [128, 2, N])
        c1H = sb("c1H", [128, 2, N + 2 * PAD], F32R)
        c1L = sb("c1L", [128, 2, N + 2 * PAD], F32R)
        ms = sb("ms", [128, 4, 132])
        msg = sb("msg", [128, 4, D])
        feat = sb("feat", [128, 4, 128])
        sq = sb("sq", [128, 4, S3])
        sqa = sb("sqa", [128, 4])
        sqb = sb("sqb", [128, 4])
        nsq = sb("nsq", [128, 4])
        lT = sb("lT", [32, 4, 128], F32R)
        rT = sb("rT", [32, 4, 128], F32R)
        adjT = sb("adjT", [128, 2, 2, N])
        aff = sb("aff", [128, 2, 2, N])
        affm = sb("affm", [128, 2, 2, N])
        nmpT = sb("nmpT", [128, 2 * N])

        xcp = sb("xcp", [128, 2 * N])
        xcT = sb("xcT", [128, 2 * N])
        tr = sb("tr", [128, 2 * N])
        tz = sb("tz", [128, 2 * N])
        nh = sb("nh", [128, 2 * N])
        rn = sb("rn", [128, 2 * N])
        npre = sb("npre", [128, 2 * N])
        ng = sb("ng", [128, 2 * N])
        hmn = sb("hmn", [128, 2 * N])
        zw = sb("zw", [128, 2 * N])
        og = sb("og", [128, 2 * N])
        x2 = sb("x2", [128, 2, 4, D])

        S = [ctx.enter_context(nc.psum_tensor(f"short{i}", [128, 512], F32)) for i in range(3)]
        P_conv2 = ctx.enter_context(nc.psum_tensor("P_conv2", [128, 512], F32))
        P_gate = [ctx.enter_context(nc.psum_tensor(f"P_gate{i}", [128, 512], F32)) for i in range(4)]
        P_r, P_z, P_ni, P_nh = P_gate
        P_maskT = S[0][:, :].bitcast(BF16)
        P_adjT = [S[1], S[2]]
        P_outT = S[0]
        P_zT = S[1]
        P_y = S[2]
        P_hT = S[0]
        P_c1 = S[1]
        P_ms = [S[2], S[0]]
        P_feat = S[1]
        P_dist = [S[2], S[0]]
        P_nmp = S[1]

        rows_zero = sem("rows_zero")
        rows_loaded = sem("rows_loaded")
        params_loaded = sem("params_loaded")
        ident_set = sem("ident_set")
        ident_ready = sem("ident_ready")
        pads_ready = sem("pads_ready")
        prep_full = sem("prep_full")
        prep_act = sem("prep_act")
        prep_dve = sem("prep_dve")
        prep_chain = sem("prep_chain")
        params_ready = sem("params_ready")
        asum_ready = sem("asum_ready")
        x_loaded = [sem(f"x_loaded{u}") for u in range(2)]
        adj_loaded = [sem(f"adj_loaded{u}") for u in range(2)]
        out_stored = [sem(f"out_stored{u}") for u in range(2)]
        mask_made = sem("mask_made")
        seed0_ready = sem("seed0_ready")
        rstd0_ready = sem("rstd0_ready")
        h0_ready = sem("h0_ready")
        sdiff_ready = sem("sdiff_ready")
        pexp_ready = sem("pexp_ready")
        numer_ready = sem("numer_ready")
        maskT_full = sem("maskT_full")
        maskT_ready = sem("maskT_ready")
        adjT_full = sem("adjT_full")
        adjT_ready = sem("adjT_ready")
        zT_full = sem("zT_full")
        zT_ready = sem("zT_ready")
        y_full = sem("y_full")
        y_ready = sem("y_ready")
        yneg_ready = sem("yneg_ready")
        yexp_ready = sem("yexp_ready")
        x1_ready = sem("x1_ready")
        seed1_ready = sem("seed1_ready")
        rstd1_ready = sem("rstd1_ready")
        h1_ready = sem("h1_ready")
        hT_full = sem("hT_full")
        hT_ready = sem("hT_ready")
        c1_full = sem("c1_full")
        c1_ready = sem("c1_ready")
        c1L_ready = sem("c1L_ready")
        ms_full = sem("ms_full")
        ms_ready = sem("ms_ready")
        msg_ready = sem("msg_ready")
        nsq_ready = sem("nsq_ready")
        feat_split = sem("feat_split")
        feat_right = sem("feat_right")
        feat_ready = sem("feat_ready")
        feat_full = sem("feat_full")
        lr_ready = sem("lr_ready")
        dist_full = sem("dist_full")
        aff_ready = sem("aff_ready")
        affm_ready = sem("affm_ready")
        nmp_full = sem("nmp_full")
        nmp_ready = sem("nmp_ready")
        conv2_full = sem("conv2_full")
        xcp_ready = sem("xcp_ready")
        xcT_ready = sem("xcT_ready")
        nh_full = sem("nh_full")
        nh_ready = sem("nh_ready")
        r_full = sem("r_full")
        tr_ready = sem("tr_ready")
        z_full = sem("z_full")
        tz_ready = sem("tz_ready")
        ni_full = sem("ni_full")
        npre_ready = sem("npre_ready")
        ng_ready = sem("ng_ready")
        hmn_ready = sem("hmn_ready")
        og_ready = sem("og_ready")
        outT_full = sem("outT_full")
        x2_ready = sem("x2_ready")
        front_chain = sem("front_chain")
        mid_chain = sem("mid_chain")
        back_chain = sem("back_chain")
        final_chain = sem("final_chain")
        pool0_chain = sem("pool0_chain")
        pool1_chain = sem("pool1_chain")
        poolf_chain = sem("poolf_chain")

        class Chain:

            def __init__(self, semaphore, per):
                self.sem, self.per = semaphore, per

            def start(self, pair):
                self.base, self.count = pair * self.per, 0

            def mark(self, ins):
                ins.then_inc(self.sem, 1)
                self.count += 1
                return self.base + self.count

            def end(self):
                assert self.count == self.per, (self.count, self.per)

        def steps(eng, body, loop_from=LOOP_FROM, loop_to=LOOP_TO):
            for s in range(FIRST_STEP, loop_from):
                body(s, s % 2, s // 2, s)
            with eng.Fori(loop_from // 2, loop_to // 2) as i:
                for u in range(2):
                    body(2 * i + u, u, i, None)
            for s in range(loop_to, LAST_STEP + 1):
                body(s, s % 2, s // 2, s)

        def stages(at):
            if at is None:
                return True, True, True, True
            return (0 <= at + 2 < PAIRS, 0 <= at + 1 < PAIRS, 0 <= at < PAIRS, 0 <= at - 1 < PAIRS)

        def conv2_tap(k):
            return conv2_raw[:, :].rearrange("o (i k) -> o k i", k=TAPS)[:, k, :]

        GROUPS = [[W_T for W_T in (W_sb[:, :], conv1_raw[:, :], msg_raw[:, :], "rows")],
                  [hh_raw[:, g, :] for g in range(GATES)],
                  [ih_raw[:, g // 2, (g % 2) * D:(g % 2 + 1) * D] for g in range(4)],
                  [ih_raw[:, g // 2, (g % 2) * D:(g % 2 + 1) * D] for g in range(4, 6)]]
        GROUPS += [[conv2_tap(k) for k in range(k0, min(k0 + 4, TAPS))] for k0 in range(0, TAPS, 4)]
        FIRST_CONV2 = 4
        PREP_BANKS = [S[0], S[1], S[2], P_conv2] + P_gate

        block = ctx.enter_context(nc.Block())

        @block.sync
        def _(sp):
            sp.wait_ge(rows_zero, 1)
            r = 0
            for v, n in ROWS:
                if len(v.shape) == 1:
                    v = v.rearrange("(r c) -> r c", r=n)
                elif v.shape[1] == 1:
                    v = v.rearrange("(r c) o -> r (c o)", r=n)
                sp.dma_start(rows[r:r + n, :], v).then_inc(rows_loaded, 16)
                r += n
            sp.dma_start(W_sb[:, :], W).then_inc(params_loaded, 16)
            sp.dma_start(conv1_raw[:, :], conv1_w.rearrange("o i k -> o (i k)")).then_inc(params_loaded, 16)
            sp.dma_start(msg_raw[:, :], w_msg).then_inc(params_loaded, 16)
            sp.dma_start(x_sb[:, 0], x_v[0]).then_inc(x_loaded[0], 16)
            sp.dma_start(adj_sb[:, 0], adj_v[0]).then_inc(adj_loaded[0], 16)
            sp.dma_start(hh_raw[:, :, :], w_hh.rearrange("(g o) i -> o g i", g=GATES)).then_inc(params_loaded, 16)
            sp.dma_start(ih_raw[:, :, :], w_ih.rearrange("(g o) i -> o g i", g=GATES)).then_inc(params_loaded, 16)
            sp.dma_start(conv2_raw[:, :], conv2_w.rearrange("o i k -> o (i k)")).then_inc(params_loaded, 16)
            sp.dma_start(b_ms[:, 0:D], b_msg.partition_broadcast(128)).then_inc(params_loaded, 16)
            sp.dma_start(b_ms[:, D:D + S3], b_se.partition_broadcast(128)).then_inc(params_loaded, 16)
            sp.dma_start(x_sb[:, 1], x_v[1]).then_inc(x_loaded[1], 16)
            sp.dma_start(adj_sb[:, 1], adj_v[1]).then_inc(adj_loaded[1], 16)

            def step(s, u, half, at):
                load = at is None or 2 <= at + 3 < PAIRS
                if load:
                    sp.wait_ge(adjT_full, 2 * s + 4)
                    sp.dma_start(adj_sb[:, (u + 3) % 2], adj_v[s + 3]).then_inc(adj_loaded[(u + 3) % 2], 16)
                if stages(at)[3]:
                    sp.wait_ge(x2_ready, s)
                    sp.dma_start(out_v[s - 1], x2[:, (u + 1) % 2]).then_inc(out_stored[(u + 1) % 2], 16)
                if load:
                    sp.wait_ge(x1_ready, s + 2)
                    sp.dma_start(x_sb[:, (u + 3) % 2], x_v[s + 3]).then_inc(x_loaded[(u + 3) % 2], 16)

            steps(sp, step, loop_to=PAIRS - 4)
            for stored in out_stored:
                sp.wait_ge(stored, 16 * (PAIRS // 2))

        @block.gpsimd
        def _(pool):
            pool.memset(rows[:, :], 0.0).then_inc(rows_zero, 1)
            pool.memset(ident[:, :], 0.0).then_inc(ident_set, 1)
            pool.memset(ident_b[:, :], 0.0).then_inc(ident_set, 1)
            pool.wait_ge(ident_set, 2)
            for m in (ident, ident_b):
                pool.affine_select(out=m[:, :], in_=m[:, :], compare_op=ALU.not_equal, fill=1.0, base=0,
                                   pattern=[[-1, 128]], channel_multiplier=1).then_inc(ident_ready, 1)
            for m in (c1H, c1L):
                pool.memset(m[:, :, 0:PAD].bitcast(F32), 0.0).then_inc(pads_ready, 1)
                pool.memset(m[:, :, N + PAD:N + 2 * PAD].bitcast(F32), 0.0).then_inc(pads_ready, 1)
            pool.memset(feat[:, :, :], 0.0).then_inc(pads_ready, 1)
            pool.memset(zeros[:, :], 0.0).then_inc(pads_ready, 1)
            pool.memset(three_halves[:, :], 1.5).then_inc(pads_ready, 1)
            pool.wait_ge(pads_ready, 7)
            pool.memset(feat[:, :, 14:16], 1.0).then_inc(pads_ready, 1)
            pool.memset(feat[:, :, 44:46], 1.0).then_inc(pads_ready, 1)

            def newton(chain, pair, nhvar, seed, tmp, rstd, done):
                chain.start(pair)
                yy = seed
                for it in range(3):
                    v = chain.mark(pool.tensor_tensor(tmp[:, :], yy[:, :], yy[:, :], ALU.mult))
                    pool.wait_ge(chain.sem, v)
                    v = chain.mark(pool.tensor_tensor(tmp[:, :], tmp[:, :], nhvar[:, :], ALU.mult))
                    pool.wait_ge(chain.sem, v)
                    v = chain.mark(pool.tensor_tensor(tmp[:, :], tmp[:, :], three_halves[:, :], ALU.add))
                    pool.wait_ge(chain.sem, v)
                    last = pool.tensor_tensor(rstd[:, :], yy[:, :], tmp[:, :], ALU.mult)
                    if it < 2:
                        pool.wait_ge(chain.sem, chain.mark(last))
                    yy = rstd
                last.then_inc(done, 1)
                chain.end()

            chain0, chain1, chainf = Chain(pool0_chain, 11), Chain(pool1_chain, 11), Chain(poolf_chain, 3)

            def step(s, u, half, at):
                front, mid, back, final = stages(at)
                if front:
                    pool.wait_ge(seed0_ready, s + 3)
                    newton(chain0, s + 2, nhvar0, seed0, nt0, rstd0, rstd0_ready)
                if mid:
                    q = s + 1
                    pool.wait_ge(seed1_ready, q + 1)
                    newton(chain1, q, nhvar1, seed1, nt1, rstd1, rstd1_ready)
                    chainf.start(q)
                    pool.wait_ge(ms_ready, 2 * q + 2)
                    v = chainf.mark(pool.tensor_tensor(sq[:, :, :], ms[:, :, D:D + S3], ms[:, :, D:D + S3], ALU.mult))
                    pool.wait_ge(chainf.sem, v)
                    v = chainf.mark(pool.tensor_tensor(sqa[:, :], zeros[:, :], sq[:, :, 0], ALU.subtract))
                    pool.wait_ge(chainf.sem, v)
                    v = chainf.mark(pool.tensor_tensor(sqb[:, :], sqa[:, :], sq[:, :, 1], ALU.subtract))
                    pool.wait_ge(chainf.sem, v)
                    pool.tensor_tensor(nsq[:, :], sqb[:, :], sq[:, :, 2], ALU.subtract).then_inc(nsq_ready, 1)
                    chainf.end()
                    pool.wait_ge(feat_split, q + 1)
                    parts = feat[:, :, 0:12].rearrange("p t (a k) -> p t a k", a=2)[:, :, :, 0:S3]
                    for j in range(2):
                        right = feat[:, :, 32 + 6 * j:38 + 6 * j].rearrange("p t (a k) -> p t a k", a=2)
                        last = pool.tensor_tensor(right, parts, parts, ALU.add)
                    last.then_inc(feat_right, 1)
                if back:
                    pool.wait_ge(ng_ready, s + 1)
                    pool.tensor_tensor(hmn[:, :], hT[:, u, :], ng[:, :], ALU.subtract).then_inc(hmn_ready, 1)

            steps(pool, step)

        @block.tensor
        def _(pe):
            pe.wait_ge(ident_ready, 2)
            pe.wait_ge(rows_loaded, 16 * len(ROWS))
            pe.wait_ge(params_loaded, 16 * NPARAM)
            for g, group in enumerate(GROUPS):
                if g >= len(PREP_BANKS):
                    pe.wait_ge(prep_act, g - len(PREP_BANKS) + 1)
                    pe.wait_ge(prep_dve, g - len(PREP_BANKS) + 1)
                bank = PREP_BANKS[g % len(PREP_BANKS)]
                for k, src in enumerate(group):
                    if isinstance(src, str):
                        last = pe.transpose(bank[:, 128 * k:128 * k + 32], rows[:, :], ident[0:32, 0:32])
                    else:
                        last = pe.transpose(bank[:, 128 * k:128 * (k + 1)], src, ident[:, :])
                last.then_inc(prep_full, 1)
            pe.wait_ge(asum_ready, 1)
            pe.wait_ge(prep_act, len(GROUPS))
            pe.wait_ge(prep_dve, len(GROUPS))
            pe.matmul(PREP_BANKS[0][:, 0:128], a_bc[:, :], WT[:, :], start=True, stop=True).then_inc(prep_full, 1)
            pe.wait_ge(params_ready, 2)

            def conv2(k0, k1):
                for k in range(k0, k1):
                    for w, m in ((w2H, c1H), (w2H, c1L), (w2L, c1H)):
                        first = k == 0 and m is c1H and w is w2H
                        last = pe.matmul(P_conv2[:, :].rearrange("p (b n) -> p b n", b=2), w[:, k, :],
                                         m[:, :, k:k + N], start=first,
                                         stop=(k == TAPS - 1 and w is w2L))
                return last

            def step(s, u, half, at):
                front, mid, back, final = stages(at)
                q, uq = s + 1, (u + 1) % 2
                if mid:
                    pe.wait_ge(numer_ready, q + 1)
                    if at is None or at >= 0:
                        pe.wait_ge(aff_ready, 2 * q)
                    src = numer[:, :, :].rearrange("p (b hi) (c hj) -> p b hi hj c", b=2, hj=2)
                    dst = P_maskT.rearrange("p (b hj hi c) -> p b hj hi c", b=2, hj=2, hi=2)
                    for b in range(2):
                        for hj in range(2):
                            for hi in range(2):
                                last = pe.transpose(dst[:, b, hj, hi, :], src[:, b, hi, hj, :], ident_b[:, :])
                    last.then_inc(maskT_full, 1)
                    for b in range(2):
                        if at is None or at >= 0:
                            if b == 0:
                                pe.wait_ge(nmp_ready, q)
                            else:
                                pe.wait_ge(aff_ready, 2 * q - 1)
                        for hm in range(2):
                            for hn in range(2):
                                j = 2 * hm + hn
                                last = pe.transpose(P_adjT[b][:, 128 * j:128 * (j + 1)],
                                                    adj_sb[:, uq, 2 * b + hn, 128 * hm:128 * (hm + 1)], ident[:, :])
                        last.then_inc(adjT_full, 1)
                if back:
                    pe.wait_ge(c1L_ready, s + 1)
                    if at is None or at >= 1:
                        pe.wait_ge(xcp_ready, s)
                    conv2(0, 4)
                if final:
                    pe.wait_ge(og_ready, s)
                    if mid:
                        pe.wait_ge(maskT_ready, q + 1)
                    o_v = og[:, :].rearrange("p (b c h) -> p b h c", b=2, h=2)
                    for b in range(2):
                        for h in range(2):
                            j = 2 * b + h
                            last = pe.transpose(P_outT[:, 128 * j:128 * (j + 1)], o_v[:, b, h, :], ident[:, :])
                    last.then_inc(outT_full, 1)
                if mid:
                    pe.wait_ge(maskT_ready, q + 1)
                    pe.wait_ge(h0_ready, q + 1)
                    pe.wait_ge(adjT_ready, 2 * q + 1)
                    for b in range(2):
                        n = 0
                        for hj in range(2):
                            for part in (h0H, h0L):
                                last = pe.matmul(P_zT[:, 256 * b:256 * (b + 1)], part[:, 2 * b + hj, :],
                                                 maskT[:, b, hj, :], start=(n == 0), stop=(n == 3))
                                n += 1
                    last.then_inc(zT_full, 1)
                if back:
                    conv2(4, 8)
                if mid:
                    pe.wait_ge(zT_ready, q + 1)
                    pe.wait_ge(adjT_ready, 2 * q + 2)
                    for j in range(4):
                        last = pe.matmul(P_y[:, 128 * j:128 * (j + 1)], zT[:, j, :], W_sb[:, :],
                                         start=True, stop=True)
                    last.then_inc(y_full, 1)
                if back:
                    conv2(8, TAPS).then_inc(conv2_full, 1)
                    if at is None or at >= 1:
                        pe.wait_ge(tz_ready, s)
                        pe.wait_ge(npre_ready, s)
                    for g, bank in enumerate((P_r, P_z)):
                        pe.matmul(bank[:, :], hhT[:, g, :], hT[:, u, :], start=True, stop=False)
                    pe.matmul(P_nh[:, :], hhT[:, 2, :], hT[:, u, :], start=True, stop=True).then_inc(nh_full, 1)
                if mid:
                    pe.wait_ge(h1_ready, q + 1)
                    if final:
                        pe.wait_ge(x2_ready, s)
                    for j in range(4):
                        last = pe.transpose(P_hT[:, 128 * j:128 * (j + 1)], h1[:, j, :], ident[:, :])
                    last.then_inc(hT_full, 1)
                if back:
                    pe.wait_ge(nmp_ready, s + 1)
                    pe.matmul(P_r[:, :], ihT[:, 1, :], nmpT[:, :], start=False, stop=False)
                if mid:
                    pe.wait_ge(hT_ready, q + 1)
                    pe.matmul(P_c1[:, :], w1T[:, :], hT[:, uq, :], start=True, stop=True).then_inc(c1_full, 1)
                    pe.wait_ge(y_ready, q + 1)
                    for i in range(2):
                        for j in range(2):
                            last = pe.matmul(P_ms[i][:, 132 * j:132 * (j + 1)],
                                             hT[:, uq, 128 * (2 * i + j):128 * (2 * i + j + 1)], w_ms[:, :],
                                             start=True, stop=True)
                        last.then_inc(ms_full, 1)
                if back:
                    pe.matmul(P_z[:, :], ihT[:, 3, :], nmpT[:, :], start=False, stop=False)
                    pe.matmul(P_ni[:, :], ihT[:, 5, :], nmpT[:, :], start=True, stop=False)
                    pe.wait_ge(xcT_ready, s + 1)
                    pe.matmul(P_r[:, :], ihT[:, 0, :], xcT[:, :], start=False, stop=True).then_inc(r_full, 1)
                    pe.matmul(P_z[:, :], ihT[:, 2, :], xcT[:, :], start=False, stop=True).then_inc(z_full, 1)
                if mid:
                    pe.wait_ge(feat_ready, q + 1)
                    pe.wait_ge(c1_ready, q + 1)
                    for j in range(4):
                        last = pe.transpose(P_feat[:, 128 * j:128 * (j + 1)], feat[:, j, :], ident[:, :])
                    last.then_inc(feat_full, 1)
                if back:
                    pe.matmul(P_ni[:, :], ihT[:, 4, :], xcT[:, :], start=False, stop=True).then_inc(ni_full, 1)
                if mid:
                    pe.wait_ge(lr_ready, q + 1)
                    r_v = rT[:, :, :].rearrange("k (b h) n -> k b (h n)", b=2)
                    for b in range(2):
                        for hm in range(2):
                            last = pe.matmul(P_dist[b][:, 256 * hm:256 * (hm + 1)], lT[:, 2 * b + hm, :],
                                             r_v[:, b, :], start=True, stop=True)
                        last.then_inc(dist_full, 1)
                    pe.wait_ge(msg_ready, q + 1)
                    for b in range(2):
                        pe.wait_ge(affm_ready, 2 * q + 1 + b)
                        for hm in range(2):
                            last = pe.matmul(P_nmp[:, 256 * b:256 * (b + 1)], msg[:, 2 * b + hm, :],
                                             affm[:, b, hm, :], start=(hm == 0), stop=(hm == 1))
                    last.then_inc(nmp_full, 1)

            steps(pe, step)

        @block.scalar
        def _(act):
            def copy(dst, src, scale=1.0):
                return act.activation(dst, src, ACT.Copy, scale=scale)

            for g, group in enumerate(GROUPS):
                act.wait_ge(prep_full, g + 1)
                bank = PREP_BANKS[g % len(PREP_BANKS)]
                n = 128 * len(group)
                if g == 0:
                    copy(WT[:, :], bank[:, 0:128])
                    copy(w1T[:, :], bank[:, 128:256])
                    last = copy(w_ms[:, 0:D], bank[:, 256:384])
                elif g == 1:
                    copy(hhT[:, 0:2, :], bank[:, 0:256])
                    last = copy(hhT[:, 2, :], bank[:, 256:384], scale=0.5)
                elif g < FIRST_CONV2:
                    last = copy(ihT[:, 4 * (g - 2):4 * (g - 2) + len(group), :], bank[:, 0:n])
                else:
                    k0 = 4 * (g - FIRST_CONV2)
                    last = copy(w2H[:, k0:k0 + len(group), :], bank[:, 0:n])
                last.then_inc(prep_act, 1)
            act.wait_ge(prep_full, len(GROUPS) + 1)
            copy(wa[:, :], PREP_BANKS[0][:, 0:128]).then_inc(params_ready, 1)

            def step(s, u, half, at):
                front, mid, back, final = stages(at)
                q, uq = s + 1, (u + 1) % 2
                if mid:
                    act.wait_ge(maskT_full, q + 1)
                    copy(maskT[:, :, :, :], P_maskT).then_inc(maskT_ready, 1)
                    for b in range(2):
                        act.wait_ge(adjT_full, 2 * q + 1 + b)
                        copy(adjT[:, b, :, :].rearrange("m hm (c hn) -> m hm hn c", hn=2),
                             P_adjT[b][:, :].rearrange("m (hm hn c) -> m hm hn c", hm=2, hn=2)).then_inc(adjT_ready, 1)
                    act.wait_ge(zT_full, q + 1)
                    copy(zT[:, :, :], P_zT[:, :]).then_inc(zT_ready, 1)
                    act.wait_ge(yneg_ready, q + 1)
                    act.activation(yexp[:, :], yneg[:, :], ACT.Exp).then_inc(yexp_ready, 1)
                if back:
                    act.wait_ge(xcp_ready, s + 1)
                    act.activation(xcT[:, :], xcp[:, :], ACT.Relu, bias=bnbias[:, 1:2]).then_inc(xcT_ready, 1)
                    act.wait_ge(nh_full, s + 1)
                    act.activation(nh[:, :], P_nh[:, :], ACT.Identity, bias=gate_b[:, 2:3]).then_inc(nh_ready, 1)
                if mid:
                    act.wait_ge(hT_full, q + 1)
                    copy(hT[:, uq, :].rearrange("p (b c h) -> p b h c", b=2, h=2),
                         P_hT[:, :].rearrange("p (b h c) -> p b h c", b=2, h=2)).then_inc(hT_ready, 1)
                    act.wait_ge(c1_full, q + 1)
                    act.activation(c1[:, :, :], P_c1[:, :].rearrange("p (b n) -> p b n", b=2), ACT.Relu,
                                   bias=bnbias[:, 0:1], scale=bnscale[:, 0:1])
                    act.activation(c1H[:, :, PAD:PAD + N], P_c1[:, :].rearrange("p (b n) -> p b n", b=2), ACT.Relu,
                                   bias=bnbias[:, 0:1], scale=bnscale[:, 0:1]).then_inc(c1_ready, 1)
                    act.wait_ge(ms_ready, 2 * q + 2)
                    act.activation(msg[:, :, :], ms[:, :, 0:D], ACT.Relu).then_inc(msg_ready, 1)
                if front:
                    act.wait_ge(sdiff_ready, s + 3)
                    act.activation(pexp[:, :, :], sdiff[:, :, :], ACT.Exp).then_inc(pexp_ready, 1)
                if back:
                    act.wait_ge(r_full, s + 1)
                    act.activation(tr[:, :], P_r[:, :], ACT.Tanh, bias=gate_b[:, 0:1], scale=0.5).then_inc(tr_ready, 1)
                    act.wait_ge(z_full, s + 1)
                    act.activation(tz[:, :], P_z[:, :], ACT.Tanh, bias=gate_b[:, 1:2], scale=0.5).then_inc(tz_ready, 1)
                if mid:
                    act.wait_ge(feat_full, q + 1)
                    copy(lT[:, :, :], P_feat[0:32, :])
                    copy(rT[:, :, :], P_feat[32:64, :]).then_inc(lr_ready, 1)
                    for b in range(2):
                        act.wait_ge(dist_full, 2 * q + 1 + b)
                        act.activation(aff[:, b, :, :], P_dist[b][:, :], ACT.Exp).then_inc(aff_ready, 1)
                if back:
                    act.wait_ge(npre_ready, s + 1)
                    act.activation(ng[:, :], npre[:, :], ACT.Tanh, bias=gate_b[:, 3:4]).then_inc(ng_ready, 1)
                if mid:
                    act.wait_ge(nmp_full, q + 1)
                    copy(nmpT[:, :], P_nmp[:, :]).then_inc(nmp_ready, 1)

            steps(act, step)

        @block.vector
        def _(dve):
            n = [0]

            def link(ins):
                n[0] += 1
                ins.then_inc(prep_chain, 1)
                dve.wait_ge(prep_chain, n[0])

            dve.memset(w_ms[:, 131:132], 0.0)
            dve.memset(b_ms[:, 131:132], 0.0)
            for g, group in enumerate(GROUPS):
                dve.wait_ge(prep_full, g + 1)
                bank = PREP_BANKS[g % len(PREP_BANKS)]
                if g == 0:
                    dve.wait_ge(prep_act, 1)
                    dve.tensor_copy(w_ms[:, D:D + S3], bank[:, 384:384 + S3])
                    link(dve.tensor_copy(cols[:, :], bank[:, 384:416]))
                    dve.tensor_copy(asum[:, :], cols[:, 0:1]).then_inc(prep_dve, 1)
                elif g >= FIRST_CONV2:
                    dve.wait_ge(prep_act, g + 1)
                    k0 = 4 * (g - FIRST_CONV2)
                    k1 = k0 + len(group)
                    dve.tensor_tensor(w2L[:, k0:k1, :], bank[:, 0:128 * len(group)].rearrange("p (k o) -> p k o", o=128),
                                      w2H[:, k0:k1, :].bitcast(F32), ALU.subtract).then_inc(prep_dve, 1)
                else:
                    dve.tensor_copy(junk[:, 0, g:g + 1], cols[:, 0:1]).then_inc(prep_dve, 1)
            link(dve.tensor_tensor(asum[:, :], cols[:, C_A:C_A + 1], cols[:, C_A + 1:C_A + 2], ALU.add))
            dve.tensor_copy(a_bc[:, :], asum[:, 0:1].to_broadcast([128, 128])).then_inc(asum_ready, 1)
            bn = cols[:, C_BN1:C_BN1 + 8].rearrange("p (n k) -> p k n", k=4)
            link(dve.tensor_scalar(bnv[:, :], bn[:, 3, :], EPS, None, ALU.add))
            link(dve.tensor_scalar(bnr[:, :].bitcast(I32), bnv[:, :].bitcast(I32), -0.5, RSQRT_SEED, ALU.mult, ALU.add))
            for _ in range(3):
                link(dve.scalar_tensor_tensor(bnt[:, :], bnr[:, :], -0.5, bnr[:, :], ALU.mult, ALU.mult))
                link(dve.tensor_tensor(bnt[:, :], bnt[:, :], bnv[:, :], ALU.mult))
                link(dve.scalar_tensor_tensor(bnr[:, :], bnt[:, :], 1.5, bnr[:, :], ALU.add, ALU.mult))
            link(dve.tensor_tensor(bnscale[:, :], bn[:, 0, :], bnr[:, :], ALU.mult))
            link(dve.tensor_tensor(bnt[:, :], bn[:, 2, :], bnscale[:, :], ALU.mult))
            link(dve.tensor_tensor(bnbias[:, :], bn[:, 1, :], bnt[:, :], ALU.subtract))
            link(dve.tensor_tensor(gate_b[:, 0:2], cols[:, C_IH:C_IH + 2], cols[:, C_HH:C_HH + 2], ALU.add))
            link(dve.tensor_scalar(gate_b[:, 0:2], gate_b[:, 0:2], 0.5, None, ALU.mult))
            dve.tensor_scalar(gate_b[:, 2:3], cols[:, C_HH + 2:C_HH + 3], 0.5, None, ALU.mult)
            dve.tensor_copy(gate_b[:, 3:4], cols[:, C_IH + 2:C_IH + 3]).then_inc(params_ready, 1)
            dve.wait_ge(params_ready, 2)
            dve.wait_ge(pads_ready, 9)

            cf, cm = Chain(front_chain, 16), Chain(mid_chain, 7)
            cb, ce = Chain(back_chain, 1), Chain(final_chain, 1)

            def step(s, u, half, at):
                front, mid, back, final = stages(at)
                p, up = s + 2, u
                q, uq = s + 1, (u + 1) % 2
                e, ue = s - 1, (u + 1) % 2
                if final:
                    ce.start(e)
                    dve.wait_ge(hmn_ready, e + 1)
                    dve.wait_ge(tz_ready, e + 1)
                    v = ce.mark(dve.scalar_tensor_tensor(zw[:, :], tz[:, :], 1.0, hmn[:, :], ALU.add, ALU.mult))
                    dve.wait_ge(ce.sem, v)
                    dve.scalar_tensor_tensor(og[:, :], zw[:, :], 0.5, ng[:, :], ALU.mult, ALU.add).then_inc(og_ready, 1)
                    ce.end()
                if front:
                    cf.start(p)
                    xp = x_sb[:, up]
                    dve.wait_ge(x_loaded[up], 16 * (half + 1) + 16)
                    for j in range(4):
                        v = dve.bn_stats(st0[:, j, :], xp[:, j, :])
                    v = cf.mark(v)
                    dve.wait_ge(adj_loaded[up], 16 * (half + 1) + 16)
                    for j in range(2):
                        if j == 1:
                            dve.wait_ge(cf.sem, v)
                        dve.tensor_scalar(mask[:, j, :], adj_sb[:, up, j, :], 0.0, None, ALU.is_gt, ALU.add,
                                          accum_out=deg[:, j:j + 1])
                    for j in range(4):
                        v = dve.bn_aggr(mv0[:, j, :], st0[:, j, :])
                    v = cf.mark(v)
                    dve.tensor_scalar(mask[:, 2, :], adj_sb[:, up, 2, :], 0.0, None, ALU.is_gt, ALU.add,
                                      accum_out=deg[:, 2:3])
                    dve.wait_ge(cf.sem, v)
                    v = cf.mark(dve.tensor_scalar(var0[:, :], mv0[:, :, 1], EPS, None, ALU.add))
                    dve.tensor_scalar(nhvar0[:, :], mv0[:, :, 1], EPS, -0.5, ALU.add, ALU.mult)
                    dve.tensor_scalar(mask[:, 3, :], adj_sb[:, up, 3, :], 0.0, None, ALU.is_gt, ALU.add,
                                      accum_out=deg[:, 3:4]).then_inc(mask_made, 1)
                    dve.wait_ge(cf.sem, v)
                    dve.tensor_scalar(seed0[:, :].bitcast(I32), var0[:, :].bitcast(I32), -0.5, RSQRT_SEED,
                                      ALU.mult, ALU.add).then_inc(seed0_ready, 1)
                if final:
                    dve.wait_ge(outT_full, e + 1)
                    if at is None or at >= 3:
                        dve.wait_ge(out_stored[ue], 16 * (half - 1 + u))
                    dve.tensor_tensor(x2[:, ue], P_outT[:, :].rearrange("p (j f) -> p j f", j=4), x1[:, ue],
                                      ALU.add).then_inc(x2_ready, 1)
                if front:
                    for j in range(4):
                        vg = dve.tensor_scalar(g0[:, j, :], xp[:, j, :], mv0[:, j, 0:1], 0.0, ALU.subtract, ALU.max)
                    vg = cf.mark(vg)
                    dve.wait_ge(mask_made, p + 1)
                    dve.tensor_scalar(some[:, 0, :], deg[:, :], 0.0, None, ALU.is_gt)
                    vs = cf.mark(dve.tensor_scalar(some[:, 1, :], deg[:, :], float(N), None, ALU.is_ge))
                if mid:
                    cm.start(q)
                    dve.wait_ge(y_full, q + 1)
                    dve.tensor_tensor(y[:, :].rearrange("p (j f) -> p j f", j=4),
                                      P_y[:, :].rearrange("p (j f) -> p j f", j=4),
                                      rden[:, uq, :].unsqueeze(2).to_broadcast([128, 4, D]), ALU.mult).then_inc(y_ready, 1)
                    dve.wait_ge(y_ready, q + 1)
                    dve.tensor_scalar(yneg[:, :], y[:, :], 0.0, None, ALU.min).then_inc(yneg_ready, 1)
                if front:
                    dve.wait_ge(cf.sem, vs)
                    vf = cf.mark(dve.tensor_scalar(fill[:, :, :], some[:, :, :], -1.0, -NEG, ALU.add, ALU.mult))
                    dve.wait_ge(rstd0_ready, p + 1)
                    for j in range(4):
                        v = dve.scalar_tensor_tensor(junk[:, j, :], g0[:, j, :], rstd0[:, j:j + 1], wa[:, :],
                                                     ALU.mult, ALU.mult, accum_out=srow[:, j:j + 1])
                    v = cf.mark(v)
                if mid:
                    dve.wait_ge(yexp_ready, q + 1)
                    v1 = cm.mark(dve.scalar_tensor_tensor(ysum[:, :], y[:, :], 0.0, yexp[:, :], ALU.max, ALU.add))
                if front:
                    dve.wait_ge(cf.sem, v)
                    ve = cf.mark(dve.scalar_tensor_tensor(erow[:, :], srow[:, :], ALPHA, srow[:, :], ALU.mult, ALU.max))
                if mid:
                    dve.wait_ge(cm.sem, v1)
                    dve.scalar_tensor_tensor(x1[:, uq], ysum[:, :].rearrange("p (j f) -> p j f", j=4), -1.0,
                                             x_sb[:, uq], ALU.add, ALU.add).then_inc(x1_ready, 1)
                if front:
                    dve.wait_ge(cf.sem, ve)
                    v = cf.mark(dve.tensor_tensor(cand[:, :, :], some[:, :, :],
                                                  erow[:, :].unsqueeze(1).to_broadcast([128, 2, 4]), ALU.mult))
                if mid:
                    dve.wait_ge(x1_ready, q + 1)
                    for j in range(4):
                        vm = dve.bn_stats(st1[:, j, :], x1[:, uq, j, :])
                    vm = cm.mark(vm)
                if front:
                    dve.wait_ge(cf.sem, v)
                    v = cf.mark(dve.tensor_tensor(cand[:, :, :], cand[:, :, :], fill[:, :, :], ALU.add))
                    if mid:
                        dve.wait_ge(zT_full, q + 1)
                    for j in range(2):
                        if mid and j == 1:
                            dve.wait_ge(cm.sem, vm)
                        dve.tensor_scalar(h0H[:, j, :], g0[:, j, :], rstd0[:, j:j + 1], None, ALU.mult)
                if mid:
                    if not front:
                        dve.wait_ge(cm.sem, vm)
                    for j in range(4):
                        vm = dve.bn_aggr(mv1[:, j, :], st1[:, j, :])
                    vm = cm.mark(vm)
                if front:
                    for j in range(2, 4):
                        vh = dve.tensor_scalar(h0H[:, j, :], g0[:, j, :], rstd0[:, j:j + 1], None, ALU.mult)
                    vh = cf.mark(vh)
                if mid:
                    dve.wait_ge(cm.sem, vm)
                    vm = cm.mark(dve.tensor_scalar(var1[:, :], mv1[:, :, 1], EPS, None, ALU.add))
                    dve.tensor_scalar(nhvar1[:, :], mv1[:, :, 1], EPS, -0.5, ALU.add, ALU.mult)
                if front:
                    dve.wait_ge(cf.sem, v)
                    v = cf.mark(dve.tensor_tensor(rmax[:, :], cand[:, 0, :], cand[:, 1, :], ALU.max))
                    dve.wait_ge(cf.sem, vh)
                    dve.scalar_tensor_tensor(h0L[:, 0, :], g0[:, 0, :], rstd0[:, 0:1], h0H[:, 0, :].bitcast(F32),
                                             ALU.mult, ALU.subtract)
                if mid:
                    dve.wait_ge(cm.sem, vm)
                    dve.tensor_scalar(seed1[:, :].bitcast(I32), var1[:, :].bitcast(I32), -0.5, RSQRT_SEED,
                                      ALU.mult, ALU.add).then_inc(seed1_ready, 1)
                if front:
                    for j in range(1, 4):
                        last = dve.scalar_tensor_tensor(h0L[:, j, :], g0[:, j, :], rstd0[:, j:j + 1],
                                                        h0H[:, j, :].bitcast(F32), ALU.mult, ALU.subtract)
                    last.then_inc(h0_ready, 1)
                    dve.wait_ge(cf.sem, v)
                    dve.tensor_tensor(sraw[:, 0, :], erow[:, :], rmax[:, :], ALU.subtract)
                    v = cf.mark(dve.tensor_scalar(sraw[:, 1, :], rmax[:, :], -1.0, NEG, ALU.mult, ALU.add))
                if mid:
                    for j in range(4):
                        vm = dve.tensor_scalar(g1[:, j, :], x1[:, uq, j, :], mv1[:, j, 0:1], 0.0, ALU.subtract, ALU.max)
                    vm = cm.mark(vm)
                if front:
                    dve.wait_ge(cf.sem, v)
                    dve.tensor_scalar(sdiff[:, :, :], sraw[:, :, :], 0.0, None, ALU.min).then_inc(sdiff_ready, 1)
                if back:
                    dve.wait_ge(conv2_full, s + 1)
                    dve.scalar_tensor_tensor(xcp[:, :], P_conv2[:, :], bnscale[:, 1:2], hT[:, u, :],
                                             ALU.mult, ALU.add).then_inc(xcp_ready, 1)
                if mid:
                    dve.wait_ge(rstd1_ready, q + 1)
                    dve.wait_ge(cm.sem, vm)
                    for j in range(4):
                        last = dve.tensor_scalar(h1[:, j, :], g1[:, j, :], rstd1[:, j:j + 1], None, ALU.mult)
                    last.then_inc(h1_ready, 1)
                    dve.wait_ge(c1_ready, q + 1)
                    dve.tensor_tensor(c1L[:, :, PAD:PAD + N], c1[:, :, :], c1H[:, :, PAD:PAD + N].bitcast(F32),
                                      ALU.subtract).then_inc(c1L_ready, 1)
                    for i in range(2):
                        dve.wait_ge(ms_full, 2 * q + 1 + i)
                        dve.tensor_tensor(ms[:, 2 * i:2 * i + 2, :], P_ms[i][:, 0:264].rearrange("p (j c) -> p j c", j=2),
                                          b_ms[:, :].unsqueeze(1).to_broadcast([128, 2, 132]), ALU.add).then_inc(ms_ready, 1)
                    dve.wait_ge(ms_ready, 2 * q + 2)
                    s_bc = ms[:, :, D:D + S3].unsqueeze(2).to_broadcast([128, 4, 2, S3])
                    vm = cm.mark(dve.tensor_copy(
                        feat[:, :, 0:6].rearrange("p t (a k) -> p t a k", a=2).bitcast(F32R), s_bc))
                    dve.wait_ge(cm.sem, vm)
                    dve.tensor_tensor(feat[:, :, 6:12].rearrange("p t (a k) -> p t a k", a=2), s_bc,
                                      feat[:, :, 0:6].rearrange("p t (a k) -> p t a k", a=2),
                                      ALU.subtract).then_inc(feat_split, 1)
                if front:
                    dve.wait_ge(pexp_ready, p + 1)
                    v = cf.mark(dve.tensor_tensor(pdiff[:, :], pexp[:, 0, :], pexp[:, 1, :], ALU.subtract))
                    dve.wait_ge(cf.sem, v)
                    if mid:
                        dve.wait_ge(maskT_full, q + 1)
                    for j in range(4):
                        last = dve.tensor_scalar(numer[:, j, :], mask[:, j, :], pdiff[:, j:j + 1], pexp[:, 1, j:j + 1],
                                                 ALU.mult, ALU.add)
                    last.then_inc(numer_ready, 1)
                    v = cf.mark(dve.tensor_tensor(dsum[:, :], deg[:, :], pdiff[:, :], ALU.mult))
                if mid:
                    dve.wait_ge(nsq_ready, q + 1)
                    both = feat[:, :, 12:80].rearrange("p t (a k) -> p t a k", a=2)
                    nsq_bc = nsq[:, :].unsqueeze(2).to_broadcast([128, 4, 2])
                    vm = cm.mark(dve.tensor_copy(both[:, :, :, 0].bitcast(F32R), nsq_bc))
                if front:
                    dve.wait_ge(cf.sem, v)
                    v = cf.mark(dve.scalar_tensor_tensor(den[:, :], pexp[:, 1, :], float(N), dsum[:, :], ALU.mult, ALU.add))
                if mid:
                    dve.wait_ge(feat_right, q + 1)
                    dve.wait_ge(cm.sem, vm)
                    dve.tensor_tensor(both[:, :, :, 1], nsq_bc, both[:, :, :, 0], ALU.subtract).then_inc(feat_ready, 1)
                    cm.end()
                if front:
                    dve.wait_ge(cf.sem, v)
                    dve.reciprocal(rden[:, up, :], den[:, :])
                    cf.end()
                if back:
                    cb.start(s)
                    dve.wait_ge(nh_ready, s + 1)
                    dve.wait_ge(tr_ready, s + 1)
                    v = cb.mark(dve.scalar_tensor_tensor(rn[:, :], tr[:, :], 1.0, nh[:, :], ALU.add, ALU.mult))
                if mid:
                    for b in range(2):
                        dve.wait_ge(aff_ready, 2 * q + 1 + b)
                        dve.tensor_tensor(affm[:, b, :, :], aff[:, b, :, :], adjT[:, b, :, :], ALU.mult).then_inc(affm_ready, 1)
                if back:
                    dve.wait_ge(ni_full, s + 1)
                    dve.wait_ge(cb.sem, v)
                    dve.tensor_tensor(npre[:, :], rn[:, :], P_ni[:, :], ALU.add).then_inc(npre_ready, 1)
                    cb.end()

            steps(dve, step, loop_from=LOOP_FROM + 2)


NAMES = ["x", "adj", "L0_gnn_W", "L0_gnn_a", "L1_gnn_w_se", "L1_gnn_b_se", "L1_gnn_conv1_w", "L1_gnn_bn1_g",
         "L1_gnn_bn1_b", "L1_gnn_bn1_m", "L1_gnn_bn1_v", "L1_gnn_conv2_w", "L1_gnn_bn2_g", "L1_gnn_bn2_b",
         "L1_gnn_bn2_m", "L1_gnn_bn2_v", "L1_gnn_w_msg", "L1_gnn_b_msg", "L1_gnn_w_ih", "L1_gnn_b_ih",
         "L1_gnn_w_hh", "L1_gnn_b_hh"]


def kernel(**inputs):
    import concourse.bacc as bacc
    from concourse.bass_utils import run_bass_kernel_spmd

    nc = bacc.Bacc("TRN2", target_bir_lowering=False, num_devices=1)
    arrays, args = {}, []
    for name in NAMES:
        v = np.ascontiguousarray(inputs[name])
        arrays[f"in_{name}"] = v
        args.append(nc.dram_tensor(f"in_{name}", v.shape, mybir.dt.from_np(v.dtype), kind="ExternalInput").ap())
    args.append(nc.dram_tensor("out_x", (B, N, D), F32, kind="ExternalOutput").ap())
    bass_gnn_kernel(nc, *args)
    result = run_bass_kernel_spmd(nc, [arrays], core_ids=[0])
    return result.results[0]["out_x"]
```

```python
import numpy as np
import concourse.bass as bass
from concourse import mybir
from contextlib import ExitStack

F32 = mybir.dt.float32
F32R = mybir.dt.float32r
BF16 = mybir.dt.bfloat16
I32 = mybir.dt.int32
ALU = mybir.AluOpType
ACT = mybir.ActivationFunctionType
AX = mybir.AxisListType

B, N, D = 32, 256, 128
PAIRS = B // 2
TAPS = 17
PAD = TAPS // 2
GATES = 3
S3 = 3
EPS = 1e-5
NEG = -9000000000000000.0
ALPHA = 0.2
RSQRT_SEED = 1597463007.0
FIRST_STEP, LAST_STEP = -2, PAIRS
LOOP_FROM, LOOP_TO = 2, PAIRS - 2


def bass_gnn_kernel(nc, x, adj, W, a, w_se, b_se, conv1_w, bn1_g, bn1_b, bn1_m, bn1_v, conv2_w,
                    bn2_g, bn2_b, bn2_m, bn2_v, w_msg, b_msg, w_ih, b_ih, w_hh, b_hh, out):
    x_v = x.rearrange("(t b) (p h) f -> t p b (h f)", b=2, h=2)
    adj_v = adj.rearrange("(t b) (p h) j -> t p b (h j)", b=2, h=2)
    out_v = out.rearrange("(t b) (p h) f -> t p b (h f)", b=2, h=2)

    ROWS = [(w_se, 3), (bn1_g, 1), (bn1_b, 1), (bn1_m, 1), (bn1_v, 1), (bn2_g, 1), (bn2_b, 1),
            (bn2_m, 1), (bn2_v, 1), (b_ih, 3), (b_hh, 3), (a, 2)]
    C_SE, C_BN1, C_BN2, C_IH, C_HH, C_A = 0, 3, 7, 11, 14, 17
    NPARAM = 8

    with ExitStack() as ctx:
        def sb(name, shape, dt=F32):
            return ctx.enter_context(nc.sbuf_tensor(name, shape, dt))

        def sem(name):
            return ctx.enter_context(nc.semaphore(name))

        ident = sb("ident", [128, 128])
        ident_b = sb("ident_b", [128, 128], BF16)
        rows = sb("rows", [32, 128])
        cols = sb("cols", [128, 32])
        W_sb = sb("W_sb", [128, 128])
        WT = sb("WT", [128, 128])
        conv1_raw = sb("conv1_raw", [128, 128])
        msg_raw = sb("msg_raw", [128, 128])
        ih_raw = sb("ih_raw", [128, GATES, 2 * D])
        hh_raw = sb("hh_raw", [128, GATES, D])
        conv2_raw = sb("conv2_raw", [128, D * TAPS])
        w1H = sb("w1H", [128, 128], F32R)
        w1L = sb("w1L", [128, 128], F32R)
        w_msH = sb("w_msH", [128, 132], F32R)
        w_msL = sb("w_msL", [128, 132], F32R)
        ihH = sb("ihH", [128, GATES * 2, 128], F32R)
        ihL = sb("ihL", [128, GATES * 2, 128], F32R)
        hhH = sb("hhH", [128, GATES, 128], F32R)
        hhL = sb("hhL", [128, GATES, 128], F32R)
        w2H = sb("w2H", [128, TAPS, 128], F32R)
        w2L = sb("w2L", [128, TAPS, 128], F32R)
        b_ms = sb("b_ms", [128, 132])
        a_bc = sb("a_bc", [128, 128])
        wa = sb("wa", [128, 4, 128])
        bnv = sb("bnv", [128, 2])
        bnr = sb("bnr", [128, 2])
        bnt = sb("bnt", [128, 2])
        bnscale = sb("bnscale", [128, 2])
        bnbias = sb("bnbias", [128, 2])
        gate_b = sb("gate_b", [128, 4])
        asum = sb("asum", [128, 1])

        zeros = sb("zeros", [128, 4])
        three_halves = sb("three_halves", [128, 4])

        x_sb = sb("x_sb", [128, 2, 4, D])
        adj_sb = sb("adj_sb", [128, 2, 4, N])
        st0 = sb("st0", [128, 4, 6])
        mv0 = sb("mv0", [128, 4, 2])
        var0 = sb("var0", [128, 4])
        nhvar0 = sb("nhvar0", [128, 4])
        seed0 = sb("seed0", [128, 4])
        rstd0 = sb("rstd0", [128, 4])
        nt0 = sb("nt0", [128, 4])
        nmr0 = sb("nmr0", [128, 4])
        nr0 = sb("nr0", [128, 4])
        h0 = sb("h0", [128, 4, D])
        sprod = sb("sprod", [128, 4, D])
        h0H = sb("h0H", [128, 4, D], F32R)
        h0L = sb("h0L", [128, 4, D], F32R)
        junk_b = sb("junk_b", [128, 4, N], BF16)
        mask = sb("mask", [128, 2, 4, N], BF16)
        numer = sb("numer", [128, 4, N], BF16)
        deg = sb("deg", [128, 4])
        srow = sb("srow", [128, 4])
        erow = sb("erow", [128, 4])
        some = sb("some", [128, 2, 4])
        fill = sb("fill", [128, 2, 4])
        cand = sb("cand", [128, 2, 4])
        rmax = sb("rmax", [128, 4])
        sraw = sb("sraw", [128, 2, 4])
        sdiff = sb("sdiff", [128, 2, 4])
        pexp = sb("pexp", [128, 2, 4])
        pdiff = sb("pdiff", [128, 4])
        dsum = sb("dsum", [128, 4])
        den = sb("den", [128, 4])
        rden = sb("rden", [128, 2, 4])

        maskT = sb("maskT", [128, 2, 2, 2 * D], F32R)
        zT = sb("zT", [128, 4, D])
        y = sb("y", [128, 4 * D])
        yneg = sb("yneg", [128, 4 * D])
        yexp = sb("yexp", [128, 4 * D])
        ysum = sb("ysum", [128, 4 * D])
        x1 = sb("x1", [128, 2, 4, D])
        st1 = sb("st1", [128, 4, 6])
        mv1 = sb("mv1", [128, 4, 2])
        var1 = sb("var1", [128, 4])
        seed1 = sb("seed1", [128, 4])
        rstd1 = sb("rstd1", [128, 4])
        ya1 = sb("ya1", [128, 4])
        yb1 = sb("yb1", [128, 4])
        g1 = sb("g1", [128, 4, D])
        h1 = sb("h1", [128, 4, D])
        hT = sb("hT", [128, 2, 2 * N])
        hTH = sb("hTH", [128, 2, 2 * N], F32R)
        hTL = sb("hTL", [128, 2, 2 * N], F32R)
        c1 = sb("c1", [128, 2, N])
        c1H = sb("c1H", [128, 2, N + 2 * PAD], F32R)
        c1L = sb("c1L", [128, 2, N + 2 * PAD], F32R)
        ms = sb("ms", [128, 4, 132])
        msg = sb("msg", [128, 4, D])
        feat = sb("feat", [128, 4, 128])
        sq = sb("sq", [128, 4, S3])
        nsq = sb("nsq", [128, 4])
        lT = sb("lT", [32, 4, 128], F32R)
        rT = sb("rT", [32, 4, 128], F32R)
        adjT = sb("adjT", [128, 2, 2, N])
        aff = sb("aff", [128, 2, 2, N])
        affm = sb("affm", [128, 2, 2, N])
        nmpH = sb("nmpH", [128, 2 * N], F32R)
        nmpL = sb("nmpL", [128, 2 * N], F32R)

        xcp = sb("xcp", [128, 2 * N])
        xcT = sb("xcT", [128, 2 * N])
        xcH = sb("xcH", [128, 2 * N], F32R)
        xcL = sb("xcL", [128, 2 * N], F32R)
        tr = sb("tr", [128, 2 * N])
        tz = sb("tz", [128, 2 * N])
        nh = sb("nh", [128, 2 * N])
        rn = sb("rn", [128, 2 * N])
        npre = sb("npre", [128, 2 * N])
        ng = sb("ng", [128, 2 * N])
        hmn = sb("hmn", [128, 2 * N])
        zw = sb("zw", [128, 2 * N])
        og = sb("og", [128, 2 * N])
        x2 = sb("x2", [128, 2, 4, D])

        S = [ctx.enter_context(nc.psum_tensor(f"short{i}", [128, 512], F32)) for i in range(3)]
        P_conv2 = ctx.enter_context(nc.psum_tensor("P_conv2", [128, 512], F32))
        P_gate = [ctx.enter_context(nc.psum_tensor(f"P_gate{i}", [128, 512], F32)) for i in range(4)]
        P_r, P_z, P_ni, P_nh = P_gate
        P_maskT = S[2][:, :].bitcast(BF16)
        P_nmp = S[0]
        P_adjT = [S[1], S[2]]
        P_zT = S[1]
        P_y = S[0]
        P_outT = S[2]
        P_hT = S[0]
        P_c1 = S[1]
        P_ms = [S[2], S[0]]
        P_feat = S[1]
        P_dist = [S[2], S[0]]

        rows_zero = sem("rows_zero")
        rows_loaded = sem("rows_loaded")
        params_loaded = sem("params_loaded")
        ident_set = sem("ident_set")
        ident_ready = sem("ident_ready")
        pads_ready = sem("pads_ready")
        prep_full = sem("prep_full")
        prep_act = sem("prep_act")
        prep_dve = sem("prep_dve")
        prep_chain = sem("prep_chain")
        params_ready = sem("params_ready")
        asum_ready = sem("asum_ready")
        x_loaded = [sem(f"x_loaded{u}") for u in range(2)]
        adj_loaded = [sem(f"adj_loaded{u}") for u in range(2)]
        out_stored = [sem(f"out_stored{u}") for u in range(2)]
        mask_made = sem("mask_made")
        deg_ready = sem("deg_ready")
        seed0_ready = sem("seed0_ready")
        rstd0_ready = sem("rstd0_ready")
        h0_whole = sem("h0_whole")
        h0H_ready = sem("h0H_ready")
        h0_ready = sem("h0_ready")
        sprod_ready = sem("sprod_ready")
        dsum_ready = sem("dsum_ready")
        sdiff_ready = sem("sdiff_ready")
        pexp_ready = sem("pexp_ready")
        numer_ready = sem("numer_ready")
        maskT_full = sem("maskT_full")
        maskT_ready = sem("maskT_ready")
        adjT_full = sem("adjT_full")
        adjT_ready = sem("adjT_ready")
        zT_full = sem("zT_full")
        zT_ready = sem("zT_ready")
        y_full = sem("y_full")
        y_ready = sem("y_ready")
        yneg_ready = sem("yneg_ready")
        yexp_ready = sem("yexp_ready")
        x1_ready = sem("x1_ready")
        h1_ready = sem("h1_ready")
        hT_full = sem("hT_full")
        hT_ready = sem("hT_ready")
        hT_whole = sem("hT_whole")
        hTL_ready = sem("hTL_ready")
        c1_full = sem("c1_full")
        c1_ready = sem("c1_ready")
        c1L_ready = sem("c1L_ready")
        ms_full = sem("ms_full")
        ms_ready = sem("ms_ready")
        msg_ready = sem("msg_ready")
        feat_split = sem("feat_split")
        feat_right = sem("feat_right")
        feat_ready = sem("feat_ready")
        feat_full = sem("feat_full")
        lr_ready = sem("lr_ready")
        dist_full = sem("dist_full")
        aff_ready = sem("aff_ready")
        affm_ready = sem("affm_ready")
        nmp_full = sem("nmp_full")
        nmpH_ready = sem("nmpH_ready")
        nmpL_ready = sem("nmpL_ready")
        conv2_full = sem("conv2_full")
        xcp_ready = sem("xcp_ready")
        xcH_ready = sem("xcH_ready")
        xcL_ready = sem("xcL_ready")
        nh_full = sem("nh_full")
        nh_ready = sem("nh_ready")
        r_full = sem("r_full")
        tr_ready = sem("tr_ready")
        z_full = sem("z_full")
        tz_ready = sem("tz_ready")
        ni_full = sem("ni_full")
        npre_ready = sem("npre_ready")
        ng_ready = sem("ng_ready")
        hmn_ready = sem("hmn_ready")
        og_ready = sem("og_ready")
        outT_full = sem("outT_full")
        x2_ready = sem("x2_ready")
        front_chain = sem("front_chain")
        mid_chain = sem("mid_chain")
        back_chain = sem("back_chain")
        final_chain = sem("final_chain")
        pool0_chain = sem("pool0_chain")
        pooln_chain = sem("pooln_chain")

        class Chain:

            def __init__(self, semaphore, per):
                self.sem, self.per = semaphore, per

            def start(self, pair):
                self.base, self.count = pair * self.per, 0

            def mark(self, ins):
                ins.then_inc(self.sem, 1)
                self.count += 1
                return self.base + self.count

            def end(self):
                assert self.count == self.per, (self.count, self.per)

        def steps(eng, body, loop_from=LOOP_FROM, loop_to=LOOP_TO):
            for s in range(FIRST_STEP, loop_from):
                body(s, s % 2, s // 2, s)
            with eng.Fori(loop_from // 2, loop_to // 2) as i:
                for u in range(2):
                    body(2 * i + u, u, i, None)
            for s in range(loop_to, LAST_STEP + 1):
                body(s, s % 2, s // 2, s)

        def stages(at):
            if at is None:
                return True, True, True, True
            return (0 <= at + 2 < PAIRS, 0 <= at + 1 < PAIRS, 0 <= at < PAIRS, 0 <= at - 1 < PAIRS)

        def conv2_tap(k):
            return conv2_raw[:, :].rearrange("o (i k) -> o k i", k=TAPS)[:, k, :]

        GROUPS = [[W_T for W_T in (W_sb[:, :], conv1_raw[:, :], msg_raw[:, :], "rows")],
                  [hh_raw[:, g, :] for g in range(GATES)],
                  [ih_raw[:, g // 2, (g % 2) * D:(g % 2 + 1) * D] for g in range(4)],
                  [ih_raw[:, g // 2, (g % 2) * D:(g % 2 + 1) * D] for g in range(4, 6)]]
        GROUPS += [[conv2_tap(k) for k in range(k0, min(k0 + 4, TAPS))] for k0 in range(0, TAPS, 4)]
        FIRST_CONV2 = 4
        PREP_BANKS = [S[0], S[1], S[2], P_conv2] + P_gate

        block = ctx.enter_context(nc.Block())

        @block.sync
        def _(sp):
            sp.wait_ge(rows_zero, 1)
            r = 0
            for v, n in ROWS:
                if len(v.shape) == 1:
                    v = v.rearrange("(r c) -> r c", r=n)
                elif v.shape[1] == 1:
                    v = v.rearrange("(r c) o -> r (c o)", r=n)
                sp.dma_start(rows[r:r + n, :], v).then_inc(rows_loaded, 16)
                r += n
            sp.dma_start(W_sb[:, :], W).then_inc(params_loaded, 16)
            sp.dma_start(conv1_raw[:, :], conv1_w.rearrange("o i k -> o (i k)")).then_inc(params_loaded, 16)
            sp.dma_start(msg_raw[:, :], w_msg).then_inc(params_loaded, 16)
            sp.dma_start(x_sb[:, 0], x_v[0]).then_inc(x_loaded[0], 16)
            sp.dma_start(adj_sb[:, 0], adj_v[0]).then_inc(adj_loaded[0], 16)
            sp.dma_start(hh_raw[:, :, :], w_hh.rearrange("(g o) i -> o g i", g=GATES)).then_inc(params_loaded, 16)
            sp.dma_start(ih_raw[:, :, :], w_ih.rearrange("(g o) i -> o g i", g=GATES)).then_inc(params_loaded, 16)
            sp.dma_start(conv2_raw[:, :], conv2_w.rearrange("o i k -> o (i k)")).then_inc(params_loaded, 16)
            sp.dma_start(b_ms[:, 0:D], b_msg.partition_broadcast(128)).then_inc(params_loaded, 16)
            sp.dma_start(b_ms[:, D:D + S3], b_se.partition_broadcast(128)).then_inc(params_loaded, 16)
            sp.dma_start(x_sb[:, 1], x_v[1]).then_inc(x_loaded[1], 16)
            sp.dma_start(adj_sb[:, 1], adj_v[1]).then_inc(adj_loaded[1], 16)

            def step(s, u, half, at):
                load = at is None or 2 <= at + 3 < PAIRS
                if load:
                    sp.wait_ge(adjT_full, 2 * s + 4)
                    sp.dma_start(adj_sb[:, (u + 3) % 2], adj_v[s + 3]).then_inc(adj_loaded[(u + 3) % 2], 16)
                if stages(at)[3]:
                    sp.wait_ge(x2_ready, s)
                    sp.dma_start(out_v[s - 1], x2[:, (u + 1) % 2]).then_inc(out_stored[(u + 1) % 2], 16)
                if load:
                    sp.wait_ge(x1_ready, s + 2)
                    sp.dma_start(x_sb[:, (u + 3) % 2], x_v[s + 3]).then_inc(x_loaded[(u + 3) % 2], 16)

            steps(sp, step, loop_to=PAIRS - 4)
            for stored in out_stored:
                sp.wait_ge(stored, 16 * (PAIRS // 2))

        @block.gpsimd
        def _(pool):
            pool.memset(rows[:, :], 0.0).then_inc(rows_zero, 1)
            pool.memset(ident[:, :], 0.0).then_inc(ident_set, 1)
            pool.memset(ident_b[:, :], 0.0).then_inc(ident_set, 1)
            pool.wait_ge(ident_set, 2)
            for m in (ident, ident_b):
                pool.affine_select(out=m[:, :], in_=m[:, :], compare_op=ALU.not_equal, fill=1.0, base=0,
                                   pattern=[[-1, 128]], channel_multiplier=1).then_inc(ident_ready, 1)
            for m in (c1H, c1L):
                pool.memset(m[:, :, 0:PAD].bitcast(F32), 0.0).then_inc(pads_ready, 1)
                pool.memset(m[:, :, N + PAD:N + 2 * PAD].bitcast(F32), 0.0).then_inc(pads_ready, 1)
            pool.memset(feat[:, :, :], 0.0).then_inc(pads_ready, 1)
            pool.memset(zeros[:, :], 0.0).then_inc(pads_ready, 1)
            pool.memset(three_halves[:, :], 1.5).then_inc(pads_ready, 1)
            pool.wait_ge(pads_ready, 7)
            pool.memset(feat[:, :, 14:16], 1.0).then_inc(pads_ready, 1)
            pool.memset(feat[:, :, 44:46], 1.0).then_inc(pads_ready, 1)

            chain0, chainn = Chain(pool0_chain, 13), Chain(pooln_chain, 1)

            def step(s, u, half, at):
                front, mid, back, final = stages(at)
                p, q = s + 2, s + 1
                if front:
                    chain0.start(p)
                    pool.wait_ge(seed0_ready, p + 1)
                    yy = seed0
                    for it in range(3):
                        v = chain0.mark(pool.tensor_tensor(nt0[:, :], yy[:, :], yy[:, :], ALU.mult))
                        pool.wait_ge(chain0.sem, v)
                        v = chain0.mark(pool.tensor_tensor(nt0[:, :], nt0[:, :], nhvar0[:, :], ALU.mult))
                        pool.wait_ge(chain0.sem, v)
                        v = chain0.mark(pool.tensor_tensor(nt0[:, :], nt0[:, :], three_halves[:, :], ALU.add))
                        pool.wait_ge(chain0.sem, v)
                        v = chain0.mark(pool.tensor_tensor(rstd0[:, :], yy[:, :], nt0[:, :], ALU.mult))
                        pool.wait_ge(chain0.sem, v)
                        yy = rstd0
                    v = chain0.mark(pool.tensor_tensor(nr0[:, :], zeros[:, :], rstd0[:, :], ALU.subtract))
                    pool.wait_ge(chain0.sem, v)
                    pool.tensor_tensor(nmr0[:, :], nr0[:, :], mv0[:, :, 0], ALU.mult).then_inc(rstd0_ready, 1)
                    chain0.end()
                    pool.wait_ge(h0_whole, p + 1)
                    pool.tensor_tensor(sprod[:, :, :], h0[:, :, :], wa[:, :, :], ALU.mult).then_inc(sprod_ready, 1)
                if front:
                    chainn.start(p)
                    pool.wait_ge(pexp_ready, p + 1)
                    v = chainn.mark(pool.tensor_tensor(pdiff[:, :], pexp[:, 0, :], pexp[:, 1, :], ALU.subtract))
                    chainn.end()
                    if mid:
                        pool.wait_ge(maskT_full, q + 1)
                    pool.wait_ge(chainn.sem, v)
                    pool.tensor_tensor(dsum[:, :], deg[:, :], pdiff[:, :], ALU.mult).then_inc(dsum_ready, 1)
                    for j in range(4):
                        last = pool.tensor_scalar(numer[:, j, :], mask[:, u, j, :], pdiff[:, j:j + 1], pexp[:, 1, j:j + 1],
                                                  ALU.mult, ALU.add)
                    last.then_inc(numer_ready, 1)
                if mid:
                    pool.wait_ge(feat_split, q + 1)
                    parts = feat[:, :, 0:12].rearrange("p t (a k) -> p t a k", a=2)[:, :, :, 0:S3]
                    for j in range(2):
                        right = feat[:, :, 32 + 6 * j:38 + 6 * j].rearrange("p t (a k) -> p t a k", a=2)
                        last = pool.tensor_tensor(right, parts, parts, ALU.add)
                    last.then_inc(feat_right, 1)
                if back:
                    pool.wait_ge(xcH_ready, s + 1)
                    pool.tensor_tensor(xcL[:, :], xcT[:, :], xcH[:, :].bitcast(F32), ALU.subtract).then_inc(xcL_ready, 1)
                if mid:
                    pool.wait_ge(c1_ready, q + 1)
                    pool.tensor_tensor(c1L[:, :, PAD:PAD + N], c1[:, :, :], c1H[:, :, PAD:PAD + N].bitcast(F32),
                                       ALU.subtract).then_inc(c1L_ready, 1)
                if back:
                    pool.wait_ge(ng_ready, s + 1)
                    pool.tensor_tensor(hmn[:, :], hT[:, u, :], ng[:, :], ALU.subtract).then_inc(hmn_ready, 1)

            steps(pool, step)

        @block.tensor
        def _(pe):
            pe.wait_ge(ident_ready, 2)
            pe.wait_ge(rows_loaded, 16 * len(ROWS))
            pe.wait_ge(params_loaded, 16 * NPARAM)
            for g, group in enumerate(GROUPS):
                if g >= len(PREP_BANKS):
                    pe.wait_ge(prep_act, g - len(PREP_BANKS) + 1)
                    pe.wait_ge(prep_dve, g - len(PREP_BANKS) + 1)
                bank = PREP_BANKS[g % len(PREP_BANKS)]
                for k, src in enumerate(group):
                    if isinstance(src, str):
                        last = pe.transpose(bank[:, 128 * k:128 * k + 32], rows[:, :], ident[0:32, 0:32])
                    else:
                        last = pe.transpose(bank[:, 128 * k:128 * (k + 1)], src, ident[:, :])
                last.then_inc(prep_full, 1)
            pe.wait_ge(asum_ready, 1)
            pe.wait_ge(prep_act, len(GROUPS))
            pe.wait_ge(prep_dve, len(GROUPS))
            pe.matmul(PREP_BANKS[0][:, 0:128], a_bc[:, :], WT[:, :], start=True, stop=True).then_inc(prep_full, 1)
            pe.wait_ge(params_ready, 2)

            def conv2(k0, k1):
                for k in range(k0, k1):
                    for w, m in ((w2H, c1H), (w2H, c1L), (w2L, c1H)):
                        first = k == 0 and m is c1H and w is w2H
                        last = pe.matmul(P_conv2[:, :].rearrange("p (b n) -> p b n", b=2), w[:, k, :],
                                         m[:, :, k:k + N], start=first,
                                         stop=(k == TAPS - 1 and w is w2L))
                return last

            def passes(bank, wH, wL, mH, mL, start, stop):
                pe.matmul(bank, wH, mH, start=start, stop=False)
                pe.matmul(bank, wL, mH, start=False, stop=False)
                return pe.matmul(bank, wH, mL, start=False, stop=stop)

            def gate(bank, g, source, mH, mL, start=False, stop=False):
                return passes(bank[:, :], ihH[:, 2 * g + source, :], ihL[:, 2 * g + source, :], mH, mL, start, stop)

            def step(s, u, half, at):
                front, mid, back, final = stages(at)
                q, uq = s + 1, (u + 1) % 2
                if back:
                    pe.wait_ge(c1L_ready, s + 1)
                    if at is None or at >= 1:
                        pe.wait_ge(xcp_ready, s)
                    conv2(0, 1)
                if mid:
                    pe.wait_ge(numer_ready, q + 1)
                    if at is None or at >= 0:
                        pe.wait_ge(aff_ready, 2 * q - 1)
                    src = numer[:, :, :].rearrange("p (b hi) (c hj) -> p b hi hj c", b=2, hj=2)
                    dst = P_maskT.rearrange("p (b hj hi c) -> p b hj hi c", b=2, hj=2, hi=2)
                    for b in range(2):
                        for hj in range(2):
                            for hi in range(2):
                                last = pe.transpose(dst[:, b, hj, hi, :], src[:, b, hi, hj, :], ident_b[:, :])
                    last.then_inc(maskT_full, 1)
                if back:
                    conv2(1, 2)
                def transpose_adj(b):
                    if b == 1:
                        pe.wait_ge(maskT_ready, q + 1)
                    elif at is None or at >= 0:
                        pe.wait_ge(lr_ready, q)
                    for hm in range(2):
                        for hn in range(2):
                            j = 2 * hm + hn
                            last = pe.transpose(P_adjT[b][:, 128 * j:128 * (j + 1)],
                                                adj_sb[:, uq, 2 * b + hn, 128 * hm:128 * (hm + 1)], ident[:, :])
                    last.then_inc(adjT_full, 1)

                if mid:
                    transpose_adj(0)
                if back:
                    pe.wait_ge(msg_ready, s + 1)
                    pe.wait_ge(affm_ready, 2 * s + 2)
                    for b in range(2):
                        for hm in range(2):
                            last = pe.matmul(P_nmp[:, 256 * b:256 * (b + 1)], msg[:, 2 * b + hm, :],
                                             affm[:, b, hm, :], start=(hm == 0), stop=(hm == 1))
                    last.then_inc(nmp_full, 1)
                if mid:
                    transpose_adj(1)
                    pe.wait_ge(h0_ready, q + 1)
                    pe.wait_ge(adjT_ready, 2 * q + 1)
                    for b in range(2):
                        n = 0
                        for hj in range(2):
                            for part in (h0H, h0L):
                                last = pe.matmul(P_zT[:, 256 * b:256 * (b + 1)], part[:, 2 * b + hj, :],
                                                 maskT[:, b, hj, :], start=(n == 0), stop=(n == 3))
                                n += 1
                    last.then_inc(zT_full, 1)
                if back:
                    conv2(2, 4)
                if mid:
                    pe.wait_ge(zT_ready, q + 1)
                    if back:
                        pe.wait_ge(nmpL_ready, s + 1)
                    for j in range(4):
                        last = pe.matmul(P_y[:, 128 * j:128 * (j + 1)], zT[:, j, :], W_sb[:, :],
                                         start=True, stop=True)
                    last.then_inc(y_full, 1)
                if back:
                    conv2(4, 5)
                if final:
                    pe.wait_ge(og_ready, s)
                    if mid:
                        pe.wait_ge(adjT_ready, 2 * q + 2)
                    o_v = og[:, :].rearrange("p (b c h) -> p b h c", b=2, h=2)
                    for b in range(2):
                        for h in range(2):
                            j = 2 * b + h
                            last = pe.transpose(P_outT[:, 128 * j:128 * (j + 1)], o_v[:, b, h, :], ident[:, :])
                    last.then_inc(outT_full, 1)
                if back:
                    conv2(5, TAPS - 1)
                if mid:
                    pe.wait_ge(h1_ready, q + 1)
                    for j in range(4):
                        last = pe.transpose(P_hT[:, 128 * j:128 * (j + 1)], h1[:, j, :], ident[:, :])
                    last.then_inc(hT_full, 1)
                if back:
                    conv2(TAPS - 1, TAPS).then_inc(conv2_full, 1)
                    if at is None or at >= 1:
                        pe.wait_ge(npre_ready, s)
                    for g, bank in enumerate((P_r, P_z)):
                        passes(bank[:, :], hhH[:, g, :], hhL[:, g, :], hTH[:, u, :], hTL[:, u, :], True, False)
                if mid:
                    pe.wait_ge(hT_ready, q + 1)
                    pe.matmul(P_c1[:, :], w1H[:, :], hTH[:, uq, :], start=True, stop=False)
                    pe.matmul(P_c1[:, :], w1L[:, :], hTH[:, uq, :], start=False, stop=False)
                    pe.wait_ge(hTL_ready, q + 1)
                    pe.matmul(P_c1[:, :], w1H[:, :], hTL[:, uq, :], start=False, stop=True).then_inc(c1_full, 1)
                    if final:
                        pe.wait_ge(x2_ready, s)
                    for i in range(2):
                        if i == 1:
                            pe.wait_ge(hT_whole, q + 1)
                        for j in range(2):
                            tok = slice(128 * (2 * i + j), 128 * (2 * i + j + 1))
                            last = passes(P_ms[i][:, 132 * j:132 * (j + 1)], hTH[:, uq, tok], hTL[:, uq, tok],
                                          w_msH[:, :], w_msL[:, :], True, True)
                        last.then_inc(ms_full, 1)
                if back:
                    passes(P_nh[:, :], hhH[:, 2, :], hhL[:, 2, :], hTH[:, u, :], hTL[:, u, :],
                           True, True).then_inc(nh_full, 1)
                    if not mid:
                        pe.wait_ge(nmpL_ready, s + 1)
                    gate(P_r, 0, 1, nmpH[:, :], nmpL[:, :])
                    gate(P_z, 1, 1, nmpH[:, :], nmpL[:, :])
                if mid:
                    pe.wait_ge(feat_ready, q + 1)
                    pe.wait_ge(c1_ready, q + 1)
                    for j in range(4):
                        last = pe.transpose(P_feat[:, 128 * j:128 * (j + 1)], feat[:, j, :], ident[:, :])
                    last.then_inc(feat_full, 1)
                if back:
                    gate(P_ni, 2, 1, nmpH[:, :], nmpL[:, :], start=True)
                    pe.wait_ge(xcL_ready, s + 1)
                    gate(P_r, 0, 0, xcH[:, :], xcL[:, :], stop=True).then_inc(r_full, 1)
                if mid:
                    pe.wait_ge(lr_ready, q + 1)
                    r_v = rT[:, :, :].rearrange("k (b h) n -> k b (h n)", b=2)
                    for b in range(2):
                        for hm in range(2):
                            last = pe.matmul(P_dist[b][:, 256 * hm:256 * (hm + 1)], lT[:, 2 * b + hm, :],
                                             r_v[:, b, :], start=True, stop=True)
                        last.then_inc(dist_full, 1)
                if back:
                    gate(P_z, 1, 0, xcH[:, :], xcL[:, :], stop=True).then_inc(z_full, 1)
                    gate(P_ni, 2, 0, xcH[:, :], xcL[:, :], stop=True).then_inc(ni_full, 1)

            steps(pe, step)

        @block.scalar
        def _(act):
            def copy(dst, src, scale=1.0):
                return act.activation(dst, src, ACT.Copy, scale=scale)

            for g, group in enumerate(GROUPS):
                act.wait_ge(prep_full, g + 1)
                bank = PREP_BANKS[g % len(PREP_BANKS)]
                n = 128 * len(group)
                if g == 0:
                    copy(WT[:, :], bank[:, 0:128])
                    copy(w1H[:, :], bank[:, 128:256])
                    copy(w_msH[:, D:D + S3], bank[:, 384:384 + S3])
                    last = copy(w_msH[:, 0:D], bank[:, 256:384])
                elif g == 1:
                    copy(hhH[:, 0:2, :], bank[:, 0:256])
                    last = copy(hhH[:, 2, :], bank[:, 256:384], scale=0.5)
                elif g < FIRST_CONV2:
                    last = copy(ihH[:, 4 * (g - 2):4 * (g - 2) + len(group), :], bank[:, 0:n])
                else:
                    k0 = 4 * (g - FIRST_CONV2)
                    last = copy(w2H[:, k0:k0 + len(group), :], bank[:, 0:n])
                last.then_inc(prep_act, 1)
            act.wait_ge(prep_full, len(GROUPS) + 1)
            for j in range(4):
                last = copy(wa[:, j, :], PREP_BANKS[0][:, 0:128])
            last.then_inc(params_ready, 1)

            def step(s, u, half, at):
                front, mid, back, final = stages(at)
                q, uq = s + 1, (u + 1) % 2
                if mid:
                    act.wait_ge(maskT_full, q + 1)
                    copy(maskT[:, :, :, :], P_maskT).then_inc(maskT_ready, 1)
                if mid and back:
                    act.wait_ge(affm_ready, 2 * s + 2)
                for b in range(2):
                    if mid:
                        act.wait_ge(adjT_full, 2 * q + 1 + b)
                        copy(adjT[:, b, :, :].rearrange("m hm (c hn) -> m hm hn c", hn=2),
                             P_adjT[b][:, :].rearrange("m (hm hn c) -> m hm hn c", hm=2, hn=2)).then_inc(adjT_ready, 1)
                    if back and b == 0:
                        act.wait_ge(nmp_full, s + 1)
                        copy(nmpH[:, :], P_nmp[:, :]).then_inc(nmpH_ready, 1)
                if mid:
                    act.wait_ge(zT_full, q + 1)
                    copy(zT[:, :, :], P_zT[:, :]).then_inc(zT_ready, 1)
                    act.wait_ge(yneg_ready, q + 1)
                    act.activation(yexp[:, :], yneg[:, :], ACT.Exp).then_inc(yexp_ready, 1)
                if front:
                    act.wait_ge(mask_made, s + 3)
                    for j in range(4):
                        last = act.activation(junk_b[:, j, :], mask[:, u, j, :], ACT.Copy, accum_out=deg[:, j:j + 1])
                    last.then_inc(deg_ready, 1)
                    act.wait_ge(rstd0_ready, s + 3)
                    for j in range(4):
                        last = act.activation(h0[:, j, :], x_sb[:, u, j, :], ACT.Relu, bias=nmr0[:, j:j + 1],
                                              scale=rstd0[:, j:j + 1])
                    last.then_inc(h0_whole, 1)
                    act.wait_ge(h0_whole, s + 3)
                    copy(h0H[:, :, :], h0[:, :, :]).then_inc(h0H_ready, 1)
                if mid:
                    hT_src = P_hT[:, :].rearrange("p (b h c) -> p b h c", b=2, h=2)
                    act.wait_ge(hT_full, q + 1)
                    copy(hTH[:, uq, :].rearrange("p (b c h) -> p b h c", b=2, h=2), hT_src).then_inc(hT_ready, 1)
                if front:
                    act.wait_ge(sdiff_ready, s + 3)
                    act.activation(pexp[:, :, :], sdiff[:, :, :], ACT.Exp).then_inc(pexp_ready, 1)
                if mid:
                    act.wait_ge(hTL_ready, q + 1)
                    copy(hT[:, uq, :].rearrange("p (b c h) -> p b h c", b=2, h=2), hT_src).then_inc(hT_whole, 1)
                    act.wait_ge(c1_full, q + 1)
                    act.activation(c1[:, :, :], P_c1[:, :].rearrange("p (b n) -> p b n", b=2), ACT.Relu,
                                   bias=bnbias[:, 0:1], scale=bnscale[:, 0:1])
                    act.activation(c1H[:, :, PAD:PAD + N], P_c1[:, :].rearrange("p (b n) -> p b n", b=2), ACT.Relu,
                                   bias=bnbias[:, 0:1], scale=bnscale[:, 0:1]).then_inc(c1_ready, 1)
                if back:
                    act.wait_ge(xcp_ready, s + 1)
                    act.activation(xcH[:, :], xcp[:, :], ACT.Relu, bias=bnbias[:, 1:2])
                    act.activation(xcT[:, :], xcp[:, :], ACT.Relu, bias=bnbias[:, 1:2]).then_inc(xcH_ready, 1)
                if mid:
                    act.wait_ge(ms_ready, 2 * q + 2)
                    act.activation(msg[:, :, :], ms[:, :, 0:D], ACT.Relu).then_inc(msg_ready, 1)
                if back:
                    act.wait_ge(nh_full, s + 1)
                    act.activation(nh[:, :], P_nh[:, :], ACT.Identity, bias=gate_b[:, 2:3]).then_inc(nh_ready, 1)
                if mid:
                    act.wait_ge(feat_full, q + 1)
                    copy(lT[:, :, :], P_feat[0:32, :])
                    copy(rT[:, :, :], P_feat[32:64, :]).then_inc(lr_ready, 1)
                if back:
                    act.wait_ge(r_full, s + 1)
                    act.activation(tr[:, :], P_r[:, :], ACT.Tanh, bias=gate_b[:, 0:1], scale=0.5).then_inc(tr_ready, 1)
                if mid:
                    for b in range(2):
                        act.wait_ge(dist_full, 2 * q + 1 + b)
                        act.activation(aff[:, b, :, :], P_dist[b][:, :], ACT.Exp).then_inc(aff_ready, 1)
                if back:
                    act.wait_ge(z_full, s + 1)
                    act.activation(tz[:, :], P_z[:, :], ACT.Tanh, bias=gate_b[:, 1:2], scale=0.5).then_inc(tz_ready, 1)
                    act.wait_ge(npre_ready, s + 1)
                    act.activation(ng[:, :], npre[:, :], ACT.Tanh, bias=gate_b[:, 3:4]).then_inc(ng_ready, 1)

            steps(act, step)

        @block.vector
        def _(dve):
            n = [0]

            def link(ins):
                n[0] += 1
                ins.then_inc(prep_chain, 1)
                dve.wait_ge(prep_chain, n[0])

            dve.memset(w_msH[:, 131:132].bitcast(F32), 0.0)
            dve.memset(w_msL[:, 131:132].bitcast(F32), 0.0)
            dve.memset(b_ms[:, 131:132], 0.0)
            for g, group in enumerate(GROUPS):
                dve.wait_ge(prep_full, g + 1)
                bank = PREP_BANKS[g % len(PREP_BANKS)]
                dve.wait_ge(prep_act, g + 1)
                if g == 0:
                    dve.tensor_tensor(w1L[:, :], bank[:, 128:256], w1H[:, :].bitcast(F32), ALU.subtract)
                    dve.tensor_tensor(w_msL[:, 0:D + S3], bank[:, 256:384 + S3], w_msH[:, 0:D + S3].bitcast(F32),
                                      ALU.subtract)
                    link(dve.tensor_copy(cols[:, :], bank[:, 384:416]))
                    last = dve.tensor_copy(asum[:, :], cols[:, 0:1])
                elif g == 1:
                    dve.tensor_tensor(hhL[:, 0:2, :], bank[:, 0:256].rearrange("p (k o) -> p k o", o=128),
                                      hhH[:, 0:2, :].bitcast(F32), ALU.subtract)
                    last = dve.scalar_tensor_tensor(hhL[:, 2, :], bank[:, 256:384], 0.5, hhH[:, 2, :].bitcast(F32),
                                                    ALU.mult, ALU.subtract)
                else:
                    high, low, k0 = (ihH, ihL, 4 * (g - 2)) if g < FIRST_CONV2 else (w2H, w2L, 4 * (g - FIRST_CONV2))
                    k1 = k0 + len(group)
                    last = dve.tensor_tensor(low[:, k0:k1, :], bank[:, 0:128 * len(group)].rearrange("p (k o) -> p k o", o=128),
                                             high[:, k0:k1, :].bitcast(F32), ALU.subtract)
                last.then_inc(prep_dve, 1)
            link(dve.tensor_tensor(asum[:, :], cols[:, C_A:C_A + 1], cols[:, C_A + 1:C_A + 2], ALU.add))
            dve.tensor_copy(a_bc[:, :], asum[:, 0:1].to_broadcast([128, 128])).then_inc(asum_ready, 1)
            bn = cols[:, C_BN1:C_BN1 + 8].rearrange("p (n k) -> p k n", k=4)
            link(dve.tensor_scalar(bnv[:, :], bn[:, 3, :], EPS, None, ALU.add))
            link(dve.tensor_scalar(bnr[:, :].bitcast(I32), bnv[:, :].bitcast(I32), -0.5, RSQRT_SEED, ALU.mult, ALU.add))
            for _ in range(3):
                link(dve.scalar_tensor_tensor(bnt[:, :], bnr[:, :], -0.5, bnr[:, :], ALU.mult, ALU.mult))
                link(dve.tensor_tensor(bnt[:, :], bnt[:, :], bnv[:, :], ALU.mult))
                link(dve.scalar_tensor_tensor(bnr[:, :], bnt[:, :], 1.5, bnr[:, :], ALU.add, ALU.mult))
            link(dve.tensor_tensor(bnscale[:, :], bn[:, 0, :], bnr[:, :], ALU.mult))
            link(dve.tensor_tensor(bnt[:, :], bn[:, 2, :], bnscale[:, :], ALU.mult))
            link(dve.tensor_tensor(bnbias[:, :], bn[:, 1, :], bnt[:, :], ALU.subtract))
            link(dve.tensor_tensor(gate_b[:, 0:2], cols[:, C_IH:C_IH + 2], cols[:, C_HH:C_HH + 2], ALU.add))
            link(dve.tensor_scalar(gate_b[:, 0:2], gate_b[:, 0:2], 0.5, None, ALU.mult))
            dve.tensor_scalar(gate_b[:, 2:3], cols[:, C_HH + 2:C_HH + 3], 0.5, None, ALU.mult)
            dve.tensor_copy(gate_b[:, 3:4], cols[:, C_IH + 2:C_IH + 3]).then_inc(params_ready, 1)
            dve.wait_ge(params_ready, 2)
            dve.wait_ge(pads_ready, 9)

            cf, cm = Chain(front_chain, 12), Chain(mid_chain, 19)
            cb, ce = Chain(back_chain, 1), Chain(final_chain, 1)

            def step(s, u, half, at):
                front, mid, back, final = stages(at)
                p, up = s + 2, u
                q, uq = s + 1, (u + 1) % 2
                e, ue = s - 1, (u + 1) % 2
                if front:
                    cf.start(p)
                    dve.wait_ge(x_loaded[up], 16 * (half + 1) + 16)
                    for j in range(4):
                        v = dve.bn_stats(st0[:, j, :], x_sb[:, up, j, :])
                    v = cf.mark(v)
                    dve.wait_ge(adj_loaded[up], 16 * (half + 1) + 16)
                    if at is None or at >= 0:
                        dve.wait_ge(numer_ready, p - 1)
                    dve.tensor_scalar(mask[:, up, 0:2, :], adj_sb[:, up, 0:2, :], 0.0, None, ALU.is_gt)
                    dve.wait_ge(cf.sem, v)
                    dve.tensor_scalar(mask[:, up, 2:4, :], adj_sb[:, up, 2:4, :], 0.0, None, ALU.is_gt).then_inc(mask_made, 1)
                    for j in range(4):
                        v = dve.bn_aggr(mv0[:, j, :], st0[:, j, :])
                    dve.wait_ge(cf.sem, cf.mark(v))
                    v = cf.mark(dve.tensor_scalar(var0[:, :], mv0[:, :, 1], EPS, None, ALU.add))
                    dve.tensor_scalar(nhvar0[:, :], mv0[:, :, 1], EPS, -0.5, ALU.add, ALU.mult)
                    dve.wait_ge(cf.sem, v)
                    dve.tensor_scalar(seed0[:, :].bitcast(I32), var0[:, :].bitcast(I32), -0.5, RSQRT_SEED,
                                      ALU.mult, ALU.add).then_inc(seed0_ready, 1)
                if back:
                    dve.wait_ge(nmpH_ready, s + 1)
                    dve.tensor_tensor(nmpL[:, :], P_nmp[:, :], nmpH[:, :].bitcast(F32), ALU.subtract).then_inc(nmpL_ready, 1)
                if final:
                    ce.start(e)
                    dve.wait_ge(hmn_ready, e + 1)
                    dve.wait_ge(tz_ready, e + 1)
                    v = ce.mark(dve.scalar_tensor_tensor(zw[:, :], tz[:, :], 1.0, hmn[:, :], ALU.add, ALU.mult))
                    dve.wait_ge(ce.sem, v)
                    dve.scalar_tensor_tensor(og[:, :], zw[:, :], 0.5, ng[:, :], ALU.mult, ALU.add).then_inc(og_ready, 1)
                    ce.end()
                if mid:
                    cm.start(q)
                    dve.wait_ge(y_full, q + 1)
                    dve.tensor_tensor(y[:, :].rearrange("p (j f) -> p j f", j=4),
                                      P_y[:, :].rearrange("p (j f) -> p j f", j=4),
                                      rden[:, uq, :].unsqueeze(2).to_broadcast([128, 4, D]), ALU.mult).then_inc(y_ready, 1)
                    dve.wait_ge(y_ready, q + 1)
                    dve.tensor_scalar(yneg[:, :], y[:, :], 0.0, None, ALU.min).then_inc(yneg_ready, 1)
                if final:
                    dve.wait_ge(outT_full, e + 1)
                    if at is None or at >= 3:
                        dve.wait_ge(out_stored[ue], 16 * (half - 1 + u))
                    dve.tensor_tensor(x2[:, ue], P_outT[:, :].rearrange("p (j f) -> p j f", j=4), x1[:, ue],
                                      ALU.add).then_inc(x2_ready, 1)
                if mid:
                    dve.wait_ge(yexp_ready, q + 1)
                    v = cm.mark(dve.scalar_tensor_tensor(ysum[:, :], y[:, :], 0.0, yexp[:, :], ALU.max, ALU.add))
                    dve.wait_ge(cm.sem, v)
                    dve.scalar_tensor_tensor(x1[:, uq], ysum[:, :].rearrange("p (j f) -> p j f", j=4), -1.0,
                                             x_sb[:, uq], ALU.add, ALU.add).then_inc(x1_ready, 1)
                    dve.wait_ge(x1_ready, q + 1)
                    for j in range(4):
                        v = dve.bn_stats(st1[:, j, :], x1[:, uq, j, :])
                    v = cm.mark(v)
                if front:
                    dve.wait_ge(deg_ready, p + 1)
                    dve.tensor_scalar(some[:, 0, :], deg[:, :], 0.0, None, ALU.is_gt)
                if mid:
                    dve.wait_ge(cm.sem, v)
                if front:
                    vs = cf.mark(dve.tensor_scalar(some[:, 1, :], deg[:, :], float(N), None, ALU.is_ge))
                if mid:
                    for j in range(4):
                        v = dve.bn_aggr(mv1[:, j, :], st1[:, j, :])
                    v = cm.mark(v)
                if front:
                    dve.wait_ge(cf.sem, vs)
                    vfill = cf.mark(dve.tensor_scalar(fill[:, :, :], some[:, :, :], -1.0, -NEG, ALU.add, ALU.mult))
                if mid:
                    dve.wait_ge(cm.sem, v)
                    v = cm.mark(dve.tensor_scalar(var1[:, :], mv1[:, :, 1], EPS, None, ALU.add))
                    vg = cm.mark(dve.tensor_tensor(g1[:, :, :], x1[:, uq], mv1[:, :, 0].unsqueeze(2).to_broadcast([128, 4, D]),
                                                   ALU.subtract))
                    dve.wait_ge(cm.sem, v)
                    v = cm.mark(dve.tensor_scalar(seed1[:, :].bitcast(I32), var1[:, :].bitcast(I32), -0.5, RSQRT_SEED,
                                                  ALU.mult, ALU.add))
                    for it in range(3):
                        old, new = (seed1, yb1, seed1)[it], (yb1, seed1, rstd1)[it]
                        dve.wait_ge(cm.sem, v)
                        v = cm.mark(dve.scalar_tensor_tensor(ya1[:, :], old[:, :], -0.5, old[:, :], ALU.mult, ALU.mult))
                        dve.wait_ge(cm.sem, v)
                        v = cm.mark(dve.tensor_tensor(ya1[:, :], ya1[:, :], var1[:, :], ALU.mult))
                        dve.wait_ge(cm.sem, v)
                        v = cm.mark(dve.scalar_tensor_tensor(new[:, :], ya1[:, :], 1.5, old[:, :], ALU.add, ALU.mult))
                    dve.wait_ge(cm.sem, v)
                    dve.scalar_tensor_tensor(h1[:, :, :], g1[:, :, :], 0.0,
                                             rstd1[:, :].unsqueeze(2).to_broadcast([128, 4, D]),
                                             ALU.max, ALU.mult).then_inc(h1_ready, 1)
                if front:
                    dve.wait_ge(sprod_ready, p + 1)
                    v = cf.mark(dve.reduce_sum(srow[:, :], sprod[:, :, :], AX.X))
                    dve.wait_ge(h0H_ready, p + 1)
                    dve.tensor_tensor(h0L[:, :, :], h0[:, :, :], h0H[:, :, :].bitcast(F32), ALU.subtract).then_inc(h0_ready, 1)
                    dve.wait_ge(cf.sem, v)
                    v = cf.mark(dve.scalar_tensor_tensor(erow[:, :], srow[:, :], ALPHA, srow[:, :], ALU.mult, ALU.max))
                    dve.wait_ge(cf.sem, v)
                    v = cf.mark(dve.tensor_tensor(cand[:, :, :], some[:, :, :],
                                                  erow[:, :].unsqueeze(1).to_broadcast([128, 2, 4]), ALU.mult))
                    dve.wait_ge(cf.sem, v)
                    v = cf.mark(dve.tensor_tensor(cand[:, :, :], cand[:, :, :], fill[:, :, :], ALU.add))
                    dve.wait_ge(cf.sem, v)
                    v = cf.mark(dve.tensor_tensor(rmax[:, :], cand[:, 0, :], cand[:, 1, :], ALU.max))
                    dve.wait_ge(cf.sem, v)
                    dve.tensor_tensor(sraw[:, 0, :], erow[:, :], rmax[:, :], ALU.subtract)
                    v = cf.mark(dve.tensor_scalar(sraw[:, 1, :], rmax[:, :], -1.0, NEG, ALU.mult, ALU.add))
                    dve.wait_ge(cf.sem, v)
                    dve.tensor_scalar(sdiff[:, :, :], sraw[:, :, :], 0.0, None, ALU.min).then_inc(sdiff_ready, 1)
                if mid:
                    dve.wait_ge(hT_ready, q + 1)
                    dve.tensor_tensor(hTL[:, uq, :].rearrange("p (b c h) -> p b h c", b=2, h=2),
                                      P_hT[:, :].rearrange("p (b h c) -> p b h c", b=2, h=2),
                                      hTH[:, uq, :].bitcast(F32).rearrange("p (b c h) -> p b h c", b=2, h=2),
                                      ALU.subtract).then_inc(hTL_ready, 1)
                if back:
                    dve.wait_ge(conv2_full, s + 1)
                    dve.scalar_tensor_tensor(xcp[:, :], P_conv2[:, :], bnscale[:, 1:2], hT[:, u, :],
                                             ALU.mult, ALU.add).then_inc(xcp_ready, 1)
                if mid:
                    dve.wait_ge(ms_full, 2 * q + 1)
                    dve.tensor_tensor(ms[:, 0:2, :], P_ms[0][:, 0:264].rearrange("p (j c) -> p j c", j=2),
                                      b_ms[:, :].unsqueeze(1).to_broadcast([128, 2, 132]), ALU.add).then_inc(ms_ready, 1)
                if mid:
                    dve.wait_ge(ms_full, 2 * q + 2)
                    dve.tensor_tensor(ms[:, 2:4, :], P_ms[1][:, 0:264].rearrange("p (j c) -> p j c", j=2),
                                      b_ms[:, :].unsqueeze(1).to_broadcast([128, 2, 132]), ALU.add).then_inc(ms_ready, 1)
                if mid:
                    dve.wait_ge(ms_ready, 2 * q + 2)
                    s_bc = ms[:, :, D:D + S3].unsqueeze(2).to_broadcast([128, 4, 2, S3])
                    vm = cm.mark(dve.tensor_copy(
                        feat[:, :, 0:6].rearrange("p t (a k) -> p t a k", a=2).bitcast(F32R), s_bc))
                    vq = cm.mark(dve.scalar_tensor_tensor(sq[:, :, :], ms[:, :, D:D + S3], -1.0, ms[:, :, D:D + S3],
                                                          ALU.mult, ALU.mult))
                if mid:
                    dve.wait_ge(cm.sem, vm)
                    dve.tensor_tensor(feat[:, :, 6:12].rearrange("p t (a k) -> p t a k", a=2), s_bc,
                                      feat[:, :, 0:6].rearrange("p t (a k) -> p t a k", a=2),
                                      ALU.subtract).then_inc(feat_split, 1)
                    dve.wait_ge(cm.sem, vq)
                    vq = cm.mark(dve.reduce_sum(nsq[:, :], sq[:, :, :], AX.X))
                    dve.wait_ge(cm.sem, vq)
                    both = feat[:, :, 12:80].rearrange("p t (a k) -> p t a k", a=2)
                    nsq_bc = nsq[:, :].unsqueeze(2).to_broadcast([128, 4, 2])
                    vm = cm.mark(dve.tensor_copy(both[:, :, :, 0].bitcast(F32R), nsq_bc))
                    dve.wait_ge(feat_right, q + 1)
                    dve.wait_ge(cm.sem, vm)
                    dve.tensor_tensor(both[:, :, :, 1], nsq_bc, both[:, :, :, 0], ALU.subtract).then_inc(feat_ready, 1)
                if back:
                    cb.start(s)
                    dve.wait_ge(nh_ready, s + 1)
                    dve.wait_ge(tr_ready, s + 1)
                    vr = cb.mark(dve.scalar_tensor_tensor(rn[:, :], tr[:, :], 1.0, nh[:, :], ALU.add, ALU.mult))
                    cb.end()
                if front:
                    dve.wait_ge(dsum_ready, p + 1)
                    vd = cf.mark(dve.scalar_tensor_tensor(den[:, :], pexp[:, 1, :], float(N), dsum[:, :], ALU.mult, ALU.add))
                if mid:
                    for b in range(2):
                        dve.wait_ge(aff_ready, 2 * q + 1 + b)
                        dve.tensor_tensor(affm[:, b, :, :], aff[:, b, :, :], adjT[:, b, :, :], ALU.mult).then_inc(affm_ready, 1)
                if front:
                    dve.wait_ge(cf.sem, vd)
                    dve.reciprocal(rden[:, up, :], den[:, :])
                    cf.end()
                if back:
                    dve.wait_ge(ni_full, s + 1)
                    dve.wait_ge(cb.sem, vr)
                    dve.tensor_tensor(npre[:, :], rn[:, :], P_ni[:, :], ALU.add).then_inc(npre_ready, 1)
                if mid:
                    cm.end()

            steps(dve, step, loop_from=LOOP_FROM + 2)


NAMES = ["x", "adj", "L0_gnn_W", "L0_gnn_a", "L1_gnn_w_se", "L1_gnn_b_se", "L1_gnn_conv1_w", "L1_gnn_bn1_g",
         "L1_gnn_bn1_b", "L1_gnn_bn1_m", "L1_gnn_bn1_v", "L1_gnn_conv2_w", "L1_gnn_bn2_g", "L1_gnn_bn2_b",
         "L1_gnn_bn2_m", "L1_gnn_bn2_v", "L1_gnn_w_msg", "L1_gnn_b_msg", "L1_gnn_w_ih", "L1_gnn_b_ih",
         "L1_gnn_w_hh", "L1_gnn_b_hh"]


def kernel(**inputs):
    import concourse.bacc as bacc
    from concourse.bass_utils import run_bass_kernel_spmd

    nc = bacc.Bacc("TRN2", target_bir_lowering=False, num_devices=1)
    arrays, args = {}, []
    for name in NAMES:
        v = np.ascontiguousarray(inputs[name])
        arrays[f"in_{name}"] = v
        args.append(nc.dram_tensor(f"in_{name}", v.shape, mybir.dt.from_np(v.dtype), kind="ExternalInput").ap())
    args.append(nc.dram_tensor("out_x", (B, N, D), F32, kind="ExternalOutput").ap())
    bass_gnn_kernel(nc, *args)
    result = run_bass_kernel_spmd(nc, [arrays], core_ids=[0])
    return result.results[0]["out_x"]
```

```python
import numpy as np
import concourse.bass as bass
from concourse import mybir
from contextlib import ExitStack

F32 = mybir.dt.float32
F32R = mybir.dt.float32r
BF16 = mybir.dt.bfloat16
I32 = mybir.dt.int32
ALU = mybir.AluOpType
ACT = mybir.ActivationFunctionType
AX = mybir.AxisListType

B, N, D = 32, 256, 128
PAIRS = B // 2
TAPS = 17
PAD = TAPS // 2
HALF = N // 2 + PAD
GATES = 3
S3 = 3
EPS = 1e-5
NEG = -9000000000000000.0
ALPHA = 0.2
RSQRT_SEED = 1597463007.0
FIRST_STEP, LAST_STEP = -2, PAIRS
LOOP_FROM, LOOP_TO = 2, PAIRS - 2


def bass_gnn_kernel(nc, x, adj, W, a, w_se, b_se, conv1_w, bn1_g, bn1_b, bn1_m, bn1_v, conv2_w,
                    bn2_g, bn2_b, bn2_m, bn2_v, w_msg, b_msg, w_ih, b_ih, w_hh, b_hh, out):
    x_v = x.rearrange("(t b) (p h) f -> t p b (h f)", b=2, h=2)
    adj_v = adj.rearrange("(t b) (p h) j -> t p b (h j)", b=2, h=2)
    out_v = out.rearrange("(t b) (p h) f -> t p b (h f)", b=2, h=2)

    ROWS = [(w_se, 3), (bn1_g, 1), (bn1_b, 1), (bn1_m, 1), (bn1_v, 1), (bn2_g, 1), (bn2_b, 1),
            (bn2_m, 1), (bn2_v, 1), (b_ih, 3), (b_hh, 3)]
    C_SE, C_BN1, C_BN2, C_IH, C_HH = 0, 3, 7, 11, 14

    with ExitStack() as ctx:
        def sb(name, shape, dt=F32):
            return ctx.enter_context(nc.sbuf_tensor(name, shape, dt))

        def sem(name):
            return ctx.enter_context(nc.semaphore(name))

        ident = sb("ident", [128, 128])
        ident_b = sb("ident_b", [128, 128], BF16)
        a_rows = sb("a_rows", [2, 128])
        a_cols = sb("a_cols", [128, 2])
        rows = sb("rows", [32, 128])
        cols = sb("cols", [128, 32])
        W_sb = sb("W_sb", [128, 128])
        WT = sb("WT", [128, 128])
        conv1_raw = sb("conv1_raw", [128, 128])
        msg_raw = sb("msg_raw", [128, 128])
        ih_raw = sb("ih_raw", [128, GATES, 2 * D])
        hh_raw = sb("hh_raw", [128, GATES, D])
        conv2_raw = sb("conv2_raw", [128, D * TAPS])
        w1H = sb("w1H", [128, 128], F32R)
        w1L = sb("w1L", [128, 128], F32R)
        w_msH = sb("w_msH", [128, 132], F32R)
        w_msL = sb("w_msL", [128, 132], F32R)
        ihH = sb("ihH", [128, GATES * 2, 128], F32R)
        ihL = sb("ihL", [128, GATES * 2, 128], F32R)
        hhH = sb("hhH", [128, GATES, 128], F32R)
        hhL = sb("hhL", [128, GATES, 128], F32R)
        conv2_sum = sb("conv2_sum", [128, TAPS // 2, 128])
        w2H = sb("w2H", [128, TAPS + TAPS // 2, 128], F32R)
        w2L = sb("w2L", [128, TAPS + TAPS // 2, 128], F32R)
        b_ms = sb("b_ms", [128, 132])
        a_bc = sb("a_bc", [128, 128])
        wa = sb("wa", [128, 4, 128])
        bnv = sb("bnv", [128, 2])
        bnr = sb("bnr", [128, 2])
        bnt = sb("bnt", [128, 2])
        bnscale = sb("bnscale", [128, 2])
        bnbias = sb("bnbias", [128, 2])
        gate_b = sb("gate_b", [128, 4])
        asum = sb("asum", [128, 1])

        zeros = sb("zeros", [128, 4])
        three_halves = sb("three_halves", [128, 4])

        x_sb = sb("x_sb", [128, 2, 4, D])
        adj_sb = sb("adj_sb", [128, 2, 4, N])
        st0 = sb("st0", [128, 4, 6])
        mv0 = sb("mv0", [128, 4, 2])
        var0 = sb("var0", [128, 4])
        nhvar0 = sb("nhvar0", [128, 4])
        seed0 = sb("seed0", [128, 4])
        rstd0 = sb("rstd0", [128, 4])
        nt0 = sb("nt0", [128, 4])
        nmr0 = sb("nmr0", [128, 4])
        nr0 = sb("nr0", [128, 4])
        h0 = sb("h0", [128, 4, D])
        sprod = sb("sprod", [128, 4, D])
        h0H = sb("h0H", [128, 4, D], F32R)
        h0L = sb("h0L", [128, 4, D], F32R)
        junk_b = sb("junk_b", [128, 4, N], BF16)
        mask = sb("mask", [128, 2, 4, N], BF16)
        numer = sb("numer", [128, 4, N], BF16)
        deg = sb("deg", [128, 4])
        srow = sb("srow", [128, 4])
        erow = sb("erow", [128, 4])
        some = sb("some", [128, 2, 4])
        fill = sb("fill", [128, 2, 4])
        cand = sb("cand", [128, 2, 4])
        rmax = sb("rmax", [128, 4])
        sraw = sb("sraw", [128, 2, 4])
        sdiff = sb("sdiff", [128, 2, 4])
        pexp = sb("pexp", [128, 2, 4])
        pdiff = sb("pdiff", [128, 4])
        dsum = sb("dsum", [128, 4])
        den = sb("den", [128, 4])
        rden = sb("rden", [128, 2, 4])

        maskT = sb("maskT", [128, 2, 2, 2 * D], F32R)
        zT = sb("zT", [128, 4, D])
        y = sb("y", [128, 4 * D])
        yexp = sb("yexp", [128, 4 * D])
        x1 = sb("x1", [128, 2, 4, D])
        st1 = sb("st1", [128, 4, 6])
        mv1 = sb("mv1", [128, 4, 2])
        var1 = sb("var1", [128, 4])
        seed1 = sb("seed1", [128, 4])
        rstd1 = sb("rstd1", [128, 4])
        ya1 = sb("ya1", [128, 4])
        yb1 = sb("yb1", [128, 4])
        g1 = sb("g1", [128, 4, D])
        h1 = sb("h1", [128, 4, D])
        hT = sb("hT", [128, 2, 2 * N])
        hTH = sb("hTH", [128, 2, 2 * N], F32R)
        hTL = sb("hTL", [128, 2, 2 * N], F32R)
        c1 = sb("c1", [128, 2, 2, HALF])
        oddH = sb("oddH", [128, 2, HALF], F32R)
        oddL = sb("oddL", [128, 2, HALF], F32R)
        diff = sb("diff", [128, 2, 2, HALF])
        diffH = sb("diffH", [128, 2, 2, HALF], F32R)
        diffL = sb("diffL", [128, 2, 2, HALF], F32R)
        xcu = sb("xcu", [128, 2 * N])
        ms = sb("ms", [128, 4, 132])
        msg = sb("msg", [128, 4, D])
        feat = sb("feat", [128, 4, 128])
        xsum = sb("xsum", [128, 4, D])
        eneg = sb("eneg", [128, 4, D])
        sq = sb("sq", [128, 4, S3])
        nsq = sb("nsq", [128, 4])
        lT = sb("lT", [32, 4, 128], F32R)
        rT = sb("rT", [32, 4, 128], F32R)
        adjT = sb("adjT", [128, 2, 2, 2, N])
        aff = sb("aff", [128, 2, 2, N])
        affm = sb("affm", [128, 2, 2, N])
        nmpH = sb("nmpH", [128, 2 * N], F32R)
        nmpL = sb("nmpL", [128, 2 * N], F32R)

        xcp = sb("xcp", [128, 2 * N])
        hTb = sb("hTb", [128, 2 * N])
        xcH = sb("xcH", [128, 2 * N], F32R)
        xcL = sb("xcL", [128, 2 * N], F32R)
        tr = sb("tr", [128, 2 * N])
        tz = sb("tz", [128, 2 * N])
        nh = sb("nh", [128, 2 * N])
        rn = sb("rn", [128, 2 * N])
        npre = sb("npre", [128, 2 * N])
        ng = sb("ng", [128, 2 * N])
        hmn = sb("hmn", [128, 2 * N])
        zw = sb("zw", [128, 2 * N])
        og = sb("og", [128, 2 * N])
        x2 = sb("x2", [128, 2, 4, D])

        S = [ctx.enter_context(nc.psum_tensor(f"short{i}", [128, 512], F32)) for i in range(3)]
        P_conv2 = ctx.enter_context(nc.psum_tensor("P_conv2", [128, 512], F32))
        P_gate = [ctx.enter_context(nc.psum_tensor(f"P_gate{i}", [128, 512], F32)) for i in range(4)]
        P_r, P_z, P_ni, P_nh = P_gate
        P_hT = S[0]
        P_adjT = [S[1], S[2]]
        P_maskT = P_conv2[:, :].bitcast(BF16)
        P_c1 = P_nh
        P_ms = [P_ni, S[0]]
        P_feat = S[0]
        P_zT = P_z
        P_y = S[2]
        P_dist = [S[0], S[1]]
        P_odd = P_ni
        P_outT = S[2]
        P_nmp = S[0]

        rows_zero = sem("rows_zero")
        att_loaded = sem("att_loaded")
        mid_loaded = sem("mid_loaded")
        back_loaded = sem("back_loaded")
        ident_set = sem("ident_set")
        ident_ready = sem("ident_ready")
        pads_ready = sem("pads_ready")
        prep_full = sem("prep_full")
        prep_act = sem("prep_act")
        prep_dve = sem("prep_dve")
        prep_chain = sem("prep_chain")
        wa_ready = sem("wa_ready")
        sum_ready = sem("sum_ready")
        cols_ready = sem("cols_ready")
        x_loaded = [sem(f"x_loaded{u}") for u in range(2)]
        adj_loaded = [sem(f"adj_loaded{u}") for u in range(2)]
        out_stored = [sem(f"out_stored{u}") for u in range(2)]
        mask_made = sem("mask_made")
        deg_ready = sem("deg_ready")
        seed0_ready = sem("seed0_ready")
        rstd0_ready = sem("rstd0_ready")
        h0_whole = sem("h0_whole")
        h0H_ready = sem("h0H_ready")
        h0_ready = sem("h0_ready")
        sprod_ready = sem("sprod_ready")
        dsum_ready = sem("dsum_ready")
        sdiff_ready = sem("sdiff_ready")
        pexp_ready = sem("pexp_ready")
        numer_ready = sem("numer_ready")
        maskT_full = sem("maskT_full")
        maskT_ready = sem("maskT_ready")
        adjT_full = sem("adjT_full")
        adjT_ready = sem("adjT_ready")
        zT_full = sem("zT_full")
        zT_ready = sem("zT_ready")
        y_full = sem("y_full")
        y_ready = sem("y_ready")
        yexp_ready = sem("yexp_ready")
        x1_ready = sem("x1_ready")
        h1_ready = sem("h1_ready")
        hT_full = sem("hT_full")
        hT_ready = sem("hT_ready")
        hT_whole = sem("hT_whole")
        hTL_ready = sem("hTL_ready")
        c1_full = sem("c1_full")
        c1_ready = sem("c1_ready")
        oddH_ready = sem("oddH_ready")
        oddL_ready = sem("oddL_ready")
        diff_ready = sem("diff_ready")
        diffH_ready = sem("diffH_ready")
        diffL_ready = sem("diffL_ready")
        odd_full = sem("odd_full")
        xcu_ready = sem("xcu_ready")
        ms_full = sem("ms_full")
        ms_ready = sem("ms_ready")
        msg_ready = sem("msg_ready")
        feat_split = sem("feat_split")
        feat_right = sem("feat_right")
        feat_ready = sem("feat_ready")
        feat_full = sem("feat_full")
        lr_ready = sem("lr_ready")
        dist_full = sem("dist_full")
        aff_ready = sem("aff_ready")
        affm_ready = sem("affm_ready")
        affm1_ready = sem("affm1_ready")
        nmp_full = sem("nmp_full")
        nmpH_ready = sem("nmpH_ready")
        nmpL_ready = sem("nmpL_ready")
        conv2_full = sem("conv2_full")
        hTb_ready = sem("hTb_ready")
        xcp_ready = sem("xcp_ready")
        xcH_ready = sem("xcH_ready")
        xcL_ready = sem("xcL_ready")
        nh_full = sem("nh_full")
        nh_ready = sem("nh_ready")
        r_full = sem("r_full")
        tr_ready = sem("tr_ready")
        z_full = sem("z_full")
        tz_ready = sem("tz_ready")
        ni_full = sem("ni_full")
        rn_ready = sem("rn_ready")
        npre_ready = sem("npre_ready")
        ng_ready = sem("ng_ready")
        hmn_ready = sem("hmn_ready")
        og_ready = sem("og_ready")
        outT_full = sem("outT_full")
        x2_ready = sem("x2_ready")
        front_chain = sem("front_chain")
        mid_chain = sem("mid_chain")
        back_chain = sem("back_chain")
        final_chain = sem("final_chain")
        pool0_chain = sem("pool0_chain")
        pooln_chain = sem("pooln_chain")

        class Chain:

            def __init__(self, semaphore, per):
                self.sem, self.per = semaphore, per

            def start(self, pair):
                self.base, self.count = pair * self.per, 0

            def mark(self, ins):
                ins.then_inc(self.sem, 1)
                self.count += 1
                return self.base + self.count

            def end(self):
                assert self.count == self.per, (self.count, self.per)

        def steps(eng, body, prepare=None, loop_from=LOOP_FROM, loop_to=LOOP_TO):
            for s in range(FIRST_STEP, loop_from):
                body(s, s % 2, s // 2, s)
                if prepare and s == FIRST_STEP:
                    prepare()
            with eng.Fori(loop_from // 2, loop_to // 2) as i:
                for u in range(2):
                    body(2 * i + u, u, i, None)
            for s in range(loop_to, LAST_STEP + 1):
                body(s, s % 2, s // 2, s)

        def stages(at):
            if at is None:
                return True, True, True, True
            return (0 <= at + 2 < PAIRS, 0 <= at + 1 < PAIRS, 0 <= at < PAIRS, 0 <= at - 1 < PAIRS)

        def conv2_tap(k):
            return conv2_raw[:, :].rearrange("o (i k) -> o k i", k=TAPS)[:, k, :]

        CONV2_W = [conv2_tap(k) for k in range(TAPS)] + [conv2_sum[:, a, :] for a in range(TAPS // 2)]
        CONV2_GROUPS = [(CONV2_W[k0:k0 + 4], w2H, w2L, k0) for k0 in range(0, len(CONV2_W), 4)]
        NO_SUM = TAPS // 4
        GROUPS = CONV2_GROUPS[:NO_SUM]
        GROUPS += [([hh_raw[:, g, :] for g in range(GATES)], hhH, hhL, 0)]
        GROUPS += [([ih_raw[:, g // 2, (g % 2) * D:(g % 2 + 1) * D] for g in range(g0, min(g0 + 4, 2 * GATES))],
                    ihH, ihL, g0) for g0 in range(0, 2 * GATES, 4)]
        SUM_GROUP = len(GROUPS)
        GROUPS += CONV2_GROUPS[NO_SUM:]
        PREP_BANKS = P_gate
        LAST_GROUPS = range(len(GROUPS) - len(PREP_BANKS), len(GROUPS))
        FIRST_GROUPS = range(0, LAST_GROUPS[0])
        PREP_STEP = -1
        FULL0, ACT0, DVE0 = 4, 2, 2

        block = ctx.enter_context(nc.Block())

        @block.sync
        def _(sp):
            sp.dma_start(x_sb[:, 0], x_v[0]).then_inc(x_loaded[0], 16)
            sp.dma_start(a_rows[:, :], a.rearrange("(r c) o -> r (c o)", r=2)).then_inc(att_loaded, 16)
            sp.dma_start(W_sb[:, :], W).then_inc(att_loaded, 16)
            sp.dma_start(adj_sb[:, 0], adj_v[0]).then_inc(adj_loaded[0], 16)
            sp.dma_start(conv1_raw[:, :], conv1_w.rearrange("o i k -> o (i k)")).then_inc(mid_loaded, 16)
            sp.dma_start(msg_raw[:, :], w_msg).then_inc(mid_loaded, 16)
            sp.dma_start(conv2_raw[:, :], conv2_w.rearrange("o i k -> o (i k)")).then_inc(back_loaded, 16)
            sp.wait_ge(rows_zero, 1)
            r = 0
            for v, n in ROWS:
                v = v.rearrange("(r c) -> r c", r=n) if len(v.shape) == 1 else v
                sp.dma_start(rows[r:r + n, :], v).then_inc(mid_loaded, 16)
                r += n
            sp.dma_start(b_ms[:, 0:D], b_msg.partition_broadcast(128)).then_inc(mid_loaded, 16)
            sp.dma_start(b_ms[:, D:D + S3], b_se.partition_broadcast(128)).then_inc(mid_loaded, 16)
            sp.dma_start(x_sb[:, 1], x_v[1]).then_inc(x_loaded[1], 16)
            sp.dma_start(adj_sb[:, 1], adj_v[1]).then_inc(adj_loaded[1], 16)
            sp.dma_start(hh_raw[:, :, :], w_hh.rearrange("(g o) i -> o g i", g=GATES)).then_inc(back_loaded, 16)
            sp.dma_start(ih_raw[:, :, :], w_ih.rearrange("(g o) i -> o g i", g=GATES)).then_inc(back_loaded, 16)

            def step(s, u, half, at):
                if stages(at)[3]:
                    sp.wait_ge(x2_ready, s)
                    sp.dma_start(out_v[s - 1], x2[:, (u + 1) % 2]).then_inc(out_stored[(u + 1) % 2], 16)
                if at is None or 2 <= at + 3 < PAIRS:
                    sp.wait_ge(x1_ready, s + 2)
                    sp.dma_start(adj_sb[:, (u + 3) % 2], adj_v[s + 3]).then_inc(adj_loaded[(u + 3) % 2], 16)
                    sp.dma_start(x_sb[:, (u + 3) % 2], x_v[s + 3]).then_inc(x_loaded[(u + 3) % 2], 16)

            steps(sp, step, loop_to=PAIRS - 4)
            for stored in out_stored:
                sp.wait_ge(stored, 16 * (PAIRS // 2))

        @block.gpsimd
        def _(pool):
            pool.memset(rows[:, :], 0.0).then_inc(rows_zero, 1)
            pool.memset(ident[:, :], 0.0).then_inc(ident_set, 1)
            pool.memset(ident_b[:, :], 0.0).then_inc(ident_set, 1)
            pool.wait_ge(ident_set, 2)
            for m in (ident, ident_b):
                pool.affine_select(out=m[:, :], in_=m[:, :], compare_op=ALU.not_equal, fill=1.0, base=0,
                                   pattern=[[-1, 128]], channel_multiplier=1).then_inc(ident_ready, 1)
            for m in (c1, diff):
                pool.memset(m[:, :, :, :], 0.0).then_inc(pads_ready, 1)
            pool.memset(feat[:, :, :], 0.0).then_inc(pads_ready, 1)
            pool.memset(zeros[:, :], 0.0).then_inc(pads_ready, 1)
            pool.memset(three_halves[:, :], 1.5).then_inc(pads_ready, 1)
            pool.wait_ge(pads_ready, 5)
            pool.memset(feat[:, :, 14:16], 1.0).then_inc(pads_ready, 1)
            pool.memset(feat[:, :, 44:46], 1.0).then_inc(pads_ready, 1)

            chain0, chainn = Chain(pool0_chain, 13), Chain(pooln_chain, 1)

            def step(s, u, half, at):
                front, mid, back, final = stages(at)
                p, q = s + 2, s + 1
                if final:
                    pool.wait_ge(ng_ready, s)
                    pool.tensor_tensor(hmn[:, :], hT[:, (u + 1) % 2, :], ng[:, :], ALU.subtract).then_inc(hmn_ready, 1)
                if back:
                    pool.wait_ge(c1_ready, s + 1)
                    pool.tensor_tensor(diff[:, :, 0, :], c1[:, :, 0, :], c1[:, :, 1, :], ALU.subtract)
                    pool.tensor_tensor(diff[:, :, 1, 0:HALF - 1], c1[:, :, 0, 1:HALF], c1[:, :, 1, 0:HALF - 1],
                                       ALU.subtract).then_inc(diff_ready, 1)
                    pool.wait_ge(feat_split, s + 1)
                    parts = feat[:, :, 0:12].rearrange("p t (a k) -> p t a k", a=2)[:, :, :, 0:S3]
                    for j in range(2):
                        right = feat[:, :, 32 + 6 * j:38 + 6 * j].rearrange("p t (a k) -> p t a k", a=2)
                        last = pool.tensor_tensor(right, parts, parts, ALU.add)
                    last.then_inc(feat_right, 1)
                    pool.wait_ge(diffH_ready, s + 1)
                    pool.tensor_tensor(diffL[:, :, :, :], diff[:, :, :, :], diffH[:, :, :, :].bitcast(F32),
                                      ALU.subtract).then_inc(diffL_ready, 1)
                if front:
                    chain0.start(p)
                    pool.wait_ge(seed0_ready, p + 1)
                    yy = seed0
                    for it in range(3):
                        v = chain0.mark(pool.tensor_tensor(nt0[:, :], yy[:, :], yy[:, :], ALU.mult))
                        pool.wait_ge(chain0.sem, v)
                        v = chain0.mark(pool.tensor_tensor(nt0[:, :], nt0[:, :], nhvar0[:, :], ALU.mult))
                        pool.wait_ge(chain0.sem, v)
                        v = chain0.mark(pool.tensor_tensor(nt0[:, :], nt0[:, :], three_halves[:, :], ALU.add))
                        pool.wait_ge(chain0.sem, v)
                        v = chain0.mark(pool.tensor_tensor(rstd0[:, :], yy[:, :], nt0[:, :], ALU.mult))
                        pool.wait_ge(chain0.sem, v)
                        yy = rstd0
                    v = chain0.mark(pool.tensor_tensor(nr0[:, :], zeros[:, :], rstd0[:, :], ALU.subtract))
                    pool.wait_ge(chain0.sem, v)
                    pool.tensor_tensor(nmr0[:, :], nr0[:, :], mv0[:, :, 0], ALU.mult).then_inc(rstd0_ready, 1)
                    chain0.end()
                if back:
                    pool.wait_ge(aff_ready, 2 * s + 2)
                    pool.tensor_tensor(affm[:, 1, :, :], aff[:, 1, :, :], adjT[:, u, 1, :, :], ALU.mult).then_inc(affm1_ready, 1)
                if front:
                    if at == FIRST_STEP:
                        pool.wait_ge(wa_ready, 1)
                    pool.wait_ge(h0_whole, p + 1)
                    pool.tensor_tensor(sprod[:, :, :], h0[:, :, :], wa[:, :, :], ALU.mult).then_inc(sprod_ready, 1)
                    pool.wait_ge(h0H_ready, p + 1)
                    pool.tensor_tensor(h0L[:, :, :], h0[:, :, :], h0H[:, :, :].bitcast(F32), ALU.subtract).then_inc(h0_ready, 1)
                    chainn.start(p)
                    pool.wait_ge(pexp_ready, p + 1)
                    v = chainn.mark(pool.tensor_tensor(pdiff[:, :], pexp[:, 0, :], pexp[:, 1, :], ALU.subtract))
                    chainn.end()
                    if mid:
                        pool.wait_ge(maskT_full, q + 1)
                    pool.wait_ge(chainn.sem, v)
                    pool.tensor_tensor(dsum[:, :], deg[:, :], pdiff[:, :], ALU.mult).then_inc(dsum_ready, 1)
                    for j in range(4):
                        last = pool.tensor_scalar(numer[:, j, :], mask[:, u, j, :], pdiff[:, j:j + 1], pexp[:, 1, j:j + 1],
                                                  ALU.mult, ALU.add)
                    last.then_inc(numer_ready, 1)

            def prepare():
                pool.wait_ge(back_loaded, 16 * 3)
                taps = conv2_raw[:, :].rearrange("o (i k) -> o k i", k=TAPS)[:, 0:TAPS - 1, :]
                taps = taps.rearrange("o (a h) i -> o h a i", h=2)
                pool.tensor_tensor(conv2_sum[:, :, :], taps[:, 0], taps[:, 1], ALU.add).then_inc(sum_ready, 1)

            steps(pool, step, prepare)

        @block.tensor
        def _(pe):
            pe.wait_ge(ident_ready, 2)
            pe.wait_ge(att_loaded, 32)
            pe.transpose(S[0][:, 0:128], W_sb[:, :], ident[:, :])
            pe.transpose(S[0][:, 128:130], a_rows[:, :], ident[0:2, 0:2]).then_inc(prep_full, 1)
            pe.wait_ge(prep_act, 1)
            pe.wait_ge(prep_dve, 1)
            pe.matmul(S[1][:, 0:128], a_bc[:, :], WT[:, :], start=True, stop=True).then_inc(prep_full, 1)
            pe.wait_ge(mid_loaded, 16 * (len(ROWS) + 4))
            pe.transpose(S[2][:, 0:32], rows[:, :], ident[0:32, 0:32]).then_inc(prep_full, 1)

            def prepare():
                pe.transpose(P_conv2[:, 0:128], conv1_raw[:, :], ident[:, :])
                pe.transpose(P_conv2[:, 128:256], msg_raw[:, :], ident[:, :])
                pe.transpose(P_conv2[:, 256:288], rows[:, :], ident[0:32, 0:32]).then_inc(prep_full, 1)
                prepare_back(FIRST_GROUPS)

            def prepare_back(groups):
                pe.wait_ge(back_loaded, 16 * 3)
                for g in groups:
                    if g == SUM_GROUP:
                        pe.wait_ge(sum_ready, 1)
                    if g >= len(PREP_BANKS):
                        pe.wait_ge(prep_dve, DVE0 + g - len(PREP_BANKS) + 1)
                    bank = PREP_BANKS[g % len(PREP_BANKS)]
                    for k, src in enumerate(GROUPS[g][0]):
                        last = pe.transpose(bank[:, 128 * k:128 * (k + 1)], src, ident[:, :])
                    last.then_inc(prep_full, 1)

            P_even = P_conv2[:, 0:N].rearrange("p (b n) -> p b n", b=2)
            P_next = P_conv2[:, N:2 * N].rearrange("p (b n) -> p b n", b=2)
            P_common = P_odd[:, 0:N].rearrange("p (b n) -> p b n", b=2)
            odd_src = (oddH[:, :, :], oddL[:, :, :])
            diff_src = [(diffH[:, :, c, :], diffL[:, :, c, :]) for c in range(2)]
            PARTS = [(TAPS + a if a < TAPS // 2 else TAPS - 1, odd_src, a, P_common) for a in range(TAPS // 2 + 1)]
            COMMON = len(PARTS)
            PARTS += [(2 * a, diff_src[0], a, P_even) for a in range(TAPS // 2 + 1)]
            PARTS += [(2 * a + 1, diff_src[1], a, P_next) for a in range(TAPS // 2)]

            def conv2(n0, n1):
                for n in range(n0, n1):
                    k, (high, low), a, result = PARTS[n]
                    first = n == 0 or PARTS[n - 1][3] is not result
                    end = n + 1 == len(PARTS) or PARTS[n + 1][3] is not result
                    for w, m in ((w2H, high), (w2H, low), (w2L, high)):
                        last = pe.matmul(result, w[:, k, :], m[:, :, a:a + N // 2], start=first and w is w2H and m is high,
                                         stop=end and w is w2L)
                    if n + 1 == COMMON:
                        last.then_inc(odd_full, 1)
                return last

            def passes(bank, wH, wL, mH, mL, start, stop):
                pe.matmul(bank, wH, mH, start=start, stop=False)
                pe.matmul(bank, wL, mH, start=False, stop=False)
                return pe.matmul(bank, wH, mL, start=False, stop=stop)

            def hidden(g, u):
                passes(P_gate[g][:, :], hhH[:, g, :], hhL[:, g, :], hTH[:, u, :], hTL[:, u, :], True, False)

            def gate(bank, g, source, mH, mL, start=False, stop=False):
                return passes(bank[:, :], ihH[:, 2 * g + source, :], ihL[:, 2 * g + source, :], mH, mL, start, stop)

            def step(s, u, half, at):
                front, mid, back, final = stages(at)
                q, uq = s + 1, (u + 1) % 2
                if back:
                    pe.wait_ge(h1_ready, s + 1)
                    if final:
                        pe.wait_ge(nmpL_ready, s)
                    for j in range(4):
                        last = pe.transpose(P_hT[:, 128 * j:128 * (j + 1)], h1[:, j, :], ident[:, :])
                    last.then_inc(hT_full, 1)
                if mid:
                    if at == PREP_STEP:
                        pe.wait_ge(wa_ready, 1)
                        pe.wait_ge(cols_ready, 1)
                    for b in range(2):
                        if final:
                            if b == 0:
                                pe.wait_ge(aff_ready, 2 * s)
                            elif at is None or at >= 2:
                                pe.wait_ge(x2_ready, s - 1)
                        for hm in range(2):
                            for hn in range(2):
                                j = 2 * hm + hn
                                last = pe.transpose(P_adjT[b][:, 128 * j:128 * (j + 1)],
                                                    adj_sb[:, uq, 2 * b + hn, 128 * hm:128 * (hm + 1)], ident[:, :])
                        last.then_inc(adjT_full, 1)
                    pe.wait_ge(numer_ready, q + 1)
                    if final:
                        pe.wait_ge(xcp_ready, s)
                    elif at == PREP_STEP:
                        pe.wait_ge(prep_dve, 2)
                    src = numer[:, :, :].rearrange("p (b hi) (c hj) -> p b hi hj c", b=2, hj=2)
                    dst = P_maskT.rearrange("p (b hj hi c) -> p b hj hi c", b=2, hj=2, hi=2)
                    for b in range(2):
                        for hj in range(2):
                            for hi in range(2):
                                last = pe.transpose(dst[:, b, hj, hi, :], src[:, b, hi, hj, :], ident_b[:, :])
                    last.then_inc(maskT_full, 1)
                if back:
                    if at == PREP_STEP + 1:
                        pe.wait_ge(prep_dve, DVE0 + len(GROUPS))
                    if final:
                        pe.wait_ge(npre_ready, s)
                    pe.wait_ge(hT_ready, s + 1)
                    pe.matmul(P_c1[:, :], w1H[:, :], hTH[:, u, :], start=True, stop=False)
                    pe.matmul(P_c1[:, :], w1L[:, :], hTH[:, u, :], start=False, stop=False)
                    pe.wait_ge(hTL_ready, s + 1)
                    pe.matmul(P_c1[:, :], w1H[:, :], hTL[:, u, :], start=False, stop=True).then_inc(c1_full, 1)
                    for i in range(2):
                        if i == 1:
                            pe.wait_ge(hT_whole, s + 1)
                        for j in range(2):
                            tok = slice(128 * (2 * i + j), 128 * (2 * i + j + 1))
                            last = passes(P_ms[i][:, 132 * j:132 * (j + 1)], hTH[:, u, tok], hTL[:, u, tok],
                                          w_msH[:, :], w_msL[:, :], True, True)
                        last.then_inc(ms_full, 1)
                    hidden(0, u)
                if mid:
                    pe.wait_ge(maskT_ready, q + 1)
                    pe.wait_ge(h0_ready, q + 1)
                    if at == PREP_STEP:
                        pe.wait_ge(prep_dve, DVE0 + len(FIRST_GROUPS))
                    for b in range(2):
                        n = 0
                        for hj in range(2):
                            for part in (h0H, h0L):
                                last = pe.matmul(P_zT[:, 256 * b:256 * (b + 1)], part[:, 2 * b + hj, :],
                                                 maskT[:, b, hj, :], start=(n == 0), stop=(n == 3))
                                n += 1
                    last.then_inc(zT_full, 1)
                if back:
                    pe.wait_ge(c1_ready, s + 1)
                    passes(P_nh[:, :], hhH[:, 2, :], hhL[:, 2, :], hTH[:, u, :], hTL[:, u, :],
                           True, True).then_inc(nh_full, 1)
                    pe.wait_ge(oddL_ready, s + 1)
                    pe.wait_ge(ms_ready, 2 * s + 1)
                    conv2(0, 3)
                if mid:
                    pe.wait_ge(zT_ready, q + 1)
                    pe.wait_ge(adjT_ready, 2 * q + 2)
                    for j in range(4):
                        last = pe.matmul(P_y[:, 128 * j:128 * (j + 1)], zT[:, j, :], W_sb[:, :],
                                         start=True, stop=True)
                    last.then_inc(y_full, 1)
                if back:
                    pe.wait_ge(feat_ready, s + 1)
                    for j in range(4):
                        last = pe.transpose(P_feat[:, 128 * j:128 * (j + 1)], feat[:, j, :], ident[:, :])
                    last.then_inc(feat_full, 1)
                    conv2(3, 8)
                if at == PREP_STEP:
                    prepare_back(LAST_GROUPS)
                if back:
                    pe.wait_ge(lr_ready, s + 1)
                    r_v = rT[:, :, :].rearrange("k (b h) n -> k b (h n)", b=2)
                    for b in range(2):
                        for hm in range(2):
                            last = pe.matmul(P_dist[b][:, 256 * hm:256 * (hm + 1)], lT[:, 2 * b + hm, :],
                                             r_v[:, b, :], start=True, stop=True)
                        last.then_inc(dist_full, 1)
                if final:
                    pe.wait_ge(og_ready, s)
                    if mid:
                        pe.wait_ge(y_ready, q + 1)
                    o_v = og[:, :].rearrange("p (b c h) -> p b h c", b=2, h=2)
                    for b in range(2):
                        for h in range(2):
                            j = 2 * b + h
                            last = pe.transpose(P_outT[:, 128 * j:128 * (j + 1)], o_v[:, b, h, :], ident[:, :])
                    last.then_inc(outT_full, 1)
                if back:
                    conv2(8, COMMON)
                    pe.wait_ge(diffL_ready, s + 1)
                    conv2(COMMON, 15)
                    pe.wait_ge(msg_ready, s + 1)
                    for b in range(2):
                        pe.wait_ge((affm_ready, affm1_ready)[b], s + 1)
                        for hm in range(2):
                            last = pe.matmul(P_nmp[:, 256 * b:256 * (b + 1)], msg[:, 2 * b + hm, :],
                                             affm[:, b, hm, :], start=(hm == 0), stop=(hm == 1))
                    last.then_inc(nmp_full, 1)
                    conv2(15, len(PARTS)).then_inc(conv2_full, 1)
                    if mid:
                        pe.wait_ge(zT_ready, q + 1)
                    hidden(1, u)
                    pe.wait_ge(nmpL_ready, s + 1)
                    gate(P_r, 0, 1, nmpH[:, :], nmpL[:, :])
                    gate(P_z, 1, 1, nmpH[:, :], nmpL[:, :])
                    pe.wait_ge(xcu_ready, s + 1)
                    gate(P_ni, 2, 1, nmpH[:, :], nmpL[:, :], start=True)
                    pe.wait_ge(xcL_ready, s + 1)
                    gate(P_r, 0, 0, xcH[:, :], xcL[:, :], stop=True).then_inc(r_full, 1)
                    gate(P_z, 1, 0, xcH[:, :], xcL[:, :], stop=True).then_inc(z_full, 1)
                    gate(P_ni, 2, 0, xcH[:, :], xcL[:, :], stop=True).then_inc(ni_full, 1)

            steps(pe, step, prepare)

        @block.scalar
        def _(act):
            def copy(dst, src, scale=1.0):
                return act.activation(dst, src, ACT.Copy, scale=scale)

            act.wait_ge(prep_full, 1)
            copy(WT[:, :], S[0][:, 0:128]).then_inc(prep_act, 1)
            act.wait_ge(prep_full, 2)
            for j in range(4):
                last = copy(wa[:, j, :], S[1][:, 0:128])
            last.then_inc(wa_ready, 1)

            def prepare():
                act.wait_ge(prep_full, 4)
                copy(w1H[:, :], P_conv2[:, 0:128])
                copy(w_msH[:, 0:D + S3], P_conv2[:, 128:256 + S3]).then_inc(prep_act, 1)
                prepare_back(FIRST_GROUPS)

            def prepare_back(groups):
                for g in groups:
                    sources, high, _, k0 = GROUPS[g]
                    bank = PREP_BANKS[g % len(PREP_BANKS)]
                    act.wait_ge(prep_full, FULL0 + g + 1)
                    if high is hhH:
                        copy(hhH[:, 0:2, :], bank[:, 0:256])
                        last = copy(hhH[:, 2, :], bank[:, 256:384], scale=0.5)
                    else:
                        last = copy(high[:, k0:k0 + len(sources), :], bank[:, 0:128 * len(sources)])
                    last.then_inc(prep_act, 1)

            def step(s, u, half, at):
                front, mid, back, final = stages(at)
                q, uq = s + 1, (u + 1) % 2
                if back:
                    act.wait_ge(hT_full, s + 1)
                    copy(hTH[:, u, :].rearrange("p (b c h) -> p b h c", b=2, h=2),
                         P_hT[:, :].rearrange("p (b h c) -> p b h c", b=2, h=2)).then_inc(hT_ready, 1)
                if final:
                    act.wait_ge(npre_ready, s)
                    act.activation(ng[:, :], npre[:, :], ACT.Tanh, bias=gate_b[:, 3:4]).then_inc(ng_ready, 1)
                if mid:
                    act.wait_ge(maskT_full, q + 1)
                    copy(maskT[:, :, :, :], P_maskT).then_inc(maskT_ready, 1)
                if back:
                    act.wait_ge(c1_full, s + 1)
                    act.activation(c1[:, :, :, PAD // 2:PAD // 2 + N // 2].rearrange("p b h i -> p b i h"),
                                   P_c1[:, :].rearrange("p (b i h) -> p b i h", b=2, h=2), ACT.Relu,
                                   bias=bnbias[:, 0:1], scale=bnscale[:, 0:1]).then_inc(c1_ready, 1)
                    act.wait_ge(c1_ready, s + 1)
                    copy(oddH[:, :, :], c1[:, :, 1, :]).then_inc(oddH_ready, 1)
                if mid:
                    for b in range(2):
                        act.wait_ge(adjT_full, 2 * q + 1 + b)
                        copy(adjT[:, uq, b, :, :].rearrange("m hm (c hn) -> m hm hn c", hn=2),
                             P_adjT[b][:, :].rearrange("m (hm hn c) -> m hm hn c", hm=2, hn=2)).then_inc(adjT_ready, 1)
                if back:
                    act.wait_ge(diff_ready, s + 1)
                    copy(diffH[:, :, :, :], diff[:, :, :, :]).then_inc(diffH_ready, 1)
                if mid:
                    act.wait_ge(zT_full, q + 1)
                    copy(zT[:, :, :], P_zT[:, :]).then_inc(zT_ready, 1)
                if front:
                    act.wait_ge(mask_made, s + 3)
                    for j in range(4):
                        last = act.activation(junk_b[:, j, :], mask[:, u, j, :], ACT.Copy, accum_out=deg[:, j:j + 1])
                    last.then_inc(deg_ready, 1)
                if back:
                    act.wait_ge(feat_full, s + 1)
                    copy(lT[:, :, :], P_feat[0:32, :])
                    copy(rT[:, :, :], P_feat[32:64, :]).then_inc(lr_ready, 1)
                if mid:
                    act.wait_ge(y_ready, q + 1)
                    act.activation(yexp[:, :], y[:, :], ACT.Exp).then_inc(yexp_ready, 1)
                if back:
                    act.wait_ge(ms_ready, 2 * s + 2)
                    act.activation(msg[:, :, :], ms[:, :, 0:D], ACT.Relu).then_inc(msg_ready, 1)
                    for b in range(2):
                        act.wait_ge(dist_full, 2 * s + 1 + b)
                        act.activation(aff[:, b, :, :], P_dist[b][:, :], ACT.Exp).then_inc(aff_ready, 1)
                if at == PREP_STEP:
                    prepare_back(LAST_GROUPS)
                if back:
                    act.wait_ge(hT_whole, s + 1)
                    act.activation(hTb[:, :], hT[:, u, :], ACT.Identity, bias=bnbias[:, 1:2]).then_inc(hTb_ready, 1)
                if front:
                    act.wait_ge(rstd0_ready, s + 3)
                    for j in range(4):
                        last = act.activation(h0[:, j, :], x_sb[:, u, j, :], ACT.Relu, bias=nmr0[:, j:j + 1],
                                              scale=rstd0[:, j:j + 1])
                    last.then_inc(h0_whole, 1)
                    act.wait_ge(h0_whole, s + 3)
                    copy(h0H[:, :, :], h0[:, :, :]).then_inc(h0H_ready, 1)
                if back:
                    act.wait_ge(nmp_full, s + 1)
                    copy(nmpH[:, :], P_nmp[:, :]).then_inc(nmpH_ready, 1)
                    act.wait_ge(nh_full, s + 1)
                    act.activation(nh[:, :], P_nh[:, :], ACT.Identity, bias=gate_b[:, 2:3]).then_inc(nh_ready, 1)
                if front:
                    act.wait_ge(sdiff_ready, s + 3)
                    act.activation(pexp[:, :, :], sdiff[:, :, :], ACT.Exp).then_inc(pexp_ready, 1)
                if back:
                    act.wait_ge(xcp_ready, s + 1)
                    act.activation(xcH[:, :], xcp[:, :], ACT.Relu).then_inc(xcH_ready, 1)
                    act.wait_ge(r_full, s + 1)
                    act.activation(tr[:, :], P_r[:, :], ACT.Tanh, bias=gate_b[:, 0:1], scale=0.5).then_inc(tr_ready, 1)
                    act.wait_ge(z_full, s + 1)
                    act.activation(tz[:, :], P_z[:, :], ACT.Tanh, bias=gate_b[:, 1:2], scale=0.5).then_inc(tz_ready, 1)

            steps(act, step, prepare)

        @block.vector
        def _(dve):
            n = [0]

            def link(ins):
                n[0] += 1
                ins.then_inc(prep_chain, 1)
                dve.wait_ge(prep_chain, n[0])

            dve.memset(w_msH[:, 131:132].bitcast(F32), 0.0)
            dve.memset(w_msL[:, 131:132].bitcast(F32), 0.0)
            dve.memset(b_ms[:, 131:132], 0.0)
            dve.wait_ge(prep_full, 1)
            dve.wait_ge(prep_act, 1)
            link(dve.tensor_copy(a_cols[:, :], S[0][:, 128:130]))
            link(dve.tensor_tensor(asum[:, :], a_cols[:, 0:1], a_cols[:, 1:2], ALU.add))
            dve.tensor_copy(a_bc[:, :], asum[:, 0:1].to_broadcast([128, 128])).then_inc(prep_dve, 1)
            def prepare_vectors():
                dve.wait_ge(pads_ready, 7)
                dve.wait_ge(prep_full, 3)
                dve.tensor_copy(cols[:, :], S[2][:, 0:32]).then_inc(cols_ready, 1)
                dve.wait_ge(cols_ready, 1)
                bn = cols[:, C_BN1:C_BN1 + 8].rearrange("p (n k) -> p k n", k=4)
                link(dve.tensor_scalar(bnv[:, :], bn[:, 3, :], EPS, None, ALU.add))
                link(dve.tensor_scalar(bnr[:, :].bitcast(I32), bnv[:, :].bitcast(I32), -0.5, RSQRT_SEED, ALU.mult, ALU.add))
                for _ in range(3):
                    link(dve.scalar_tensor_tensor(bnt[:, :], bnr[:, :], -0.5, bnr[:, :], ALU.mult, ALU.mult))
                    link(dve.tensor_tensor(bnt[:, :], bnt[:, :], bnv[:, :], ALU.mult))
                    link(dve.scalar_tensor_tensor(bnr[:, :], bnt[:, :], 1.5, bnr[:, :], ALU.add, ALU.mult))
                link(dve.tensor_tensor(bnscale[:, :], bn[:, 0, :], bnr[:, :], ALU.mult))
                link(dve.tensor_tensor(bnt[:, :], bn[:, 2, :], bnscale[:, :], ALU.mult))
                link(dve.tensor_tensor(bnbias[:, :], bn[:, 1, :], bnt[:, :], ALU.subtract))
                link(dve.tensor_tensor(gate_b[:, 0:2], cols[:, C_IH:C_IH + 2], cols[:, C_HH:C_HH + 2], ALU.add))
                link(dve.tensor_scalar(gate_b[:, 0:2], gate_b[:, 0:2], 0.5, None, ALU.mult))
                dve.tensor_scalar(gate_b[:, 2:3], cols[:, C_HH + 2:C_HH + 3], 0.5, None, ALU.mult)
                link(dve.tensor_copy(gate_b[:, 3:4], cols[:, C_IH + 2:C_IH + 3]))

            def prepare():
                dve.wait_ge(prep_full, 4)
                dve.wait_ge(prep_act, 2)
                dve.tensor_tensor(w1L[:, :], P_conv2[:, 0:128], w1H[:, :].bitcast(F32), ALU.subtract)
                dve.tensor_tensor(w_msL[:, 0:D + S3], P_conv2[:, 128:256 + S3], w_msH[:, 0:D + S3].bitcast(F32),
                                  ALU.subtract).then_inc(prep_dve, 1)
                prepare_back(FIRST_GROUPS)
            def prepare_back(groups):
                for g in groups:
                    sources, high, low, k0 = GROUPS[g]
                    bank = PREP_BANKS[g % len(PREP_BANKS)][:, :].rearrange("p (k o) -> p k o", o=128)
                    dve.wait_ge(prep_act, ACT0 + g + 1)
                    if high is hhH:
                        dve.tensor_tensor(hhL[:, 0:2, :], bank[:, 0:2, :], hhH[:, 0:2, :].bitcast(F32), ALU.subtract)
                        last = dve.scalar_tensor_tensor(hhL[:, 2, :], bank[:, 2, :], 0.5, hhH[:, 2, :].bitcast(F32),
                                                        ALU.mult, ALU.subtract)
                    else:
                        k1 = k0 + len(sources)
                        last = dve.tensor_tensor(low[:, k0:k1, :], bank[:, 0:len(sources), :],
                                                 high[:, k0:k1, :].bitcast(F32), ALU.subtract)
                    last.then_inc(prep_dve, 1)

            cf, cm = Chain(front_chain, 12), Chain(mid_chain, 16)
            cb, ce = Chain(back_chain, 4), Chain(final_chain, 1)

            def step(s, u, half, at):
                front, mid, back, final = stages(at)
                p, up = s + 2, u
                q, uq = s + 1, (u + 1) % 2
                e, ue = s - 1, (u + 1) % 2
                if final:
                    dve.wait_ge(ni_full, e + 1)
                    dve.wait_ge(rn_ready, e + 1)
                    dve.tensor_tensor(npre[:, :], rn[:, :], P_ni[:, :], ALU.add).then_inc(npre_ready, 1)
                if back:
                    cb.start(s)
                    dve.wait_ge(hT_ready, s + 1)
                    dve.tensor_tensor(hTL[:, u, :].rearrange("p (b c h) -> p b h c", b=2, h=2),
                                      P_hT[:, :].rearrange("p (b h c) -> p b h c", b=2, h=2),
                                      hTH[:, u, :].bitcast(F32).rearrange("p (b c h) -> p b h c", b=2, h=2),
                                      ALU.subtract).then_inc(hTL_ready, 1)
                    dve.tensor_copy(hT[:, u, :].rearrange("p (b c h) -> p b h c", b=2, h=2),
                                    P_hT[:, :].rearrange("p (b h c) -> p b h c", b=2, h=2)).then_inc(hT_whole, 1)
                if front:
                    cf.start(p)
                    dve.wait_ge(x_loaded[up], 16 * (half + 1) + 16)
                    for j in range(4):
                        v = dve.bn_stats(st0[:, j, :], x_sb[:, up, j, :])
                    v = cf.mark(v)
                    dve.wait_ge(adj_loaded[up], 16 * (half + 1) + 16)
                    if at is None or at >= 0:
                        dve.wait_ge(numer_ready, p - 1)
                    dve.tensor_scalar(mask[:, up, 0:2, :], adj_sb[:, up, 0:2, :], 0.0, None, ALU.is_gt)
                    dve.wait_ge(cf.sem, v)
                    dve.tensor_scalar(mask[:, up, 2:4, :], adj_sb[:, up, 2:4, :], 0.0, None, ALU.is_gt).then_inc(mask_made, 1)
                    for j in range(4):
                        v = dve.bn_aggr(mv0[:, j, :], st0[:, j, :])
                    dve.wait_ge(cf.sem, cf.mark(v))
                    v = cf.mark(dve.tensor_scalar(var0[:, :], mv0[:, :, 1], EPS, None, ALU.add))
                    dve.tensor_scalar(nhvar0[:, :], mv0[:, :, 1], EPS, -0.5, ALU.add, ALU.mult)
                    dve.wait_ge(cf.sem, v)
                    dve.tensor_scalar(seed0[:, :].bitcast(I32), var0[:, :].bitcast(I32), -0.5, RSQRT_SEED,
                                      ALU.mult, ALU.add).then_inc(seed0_ready, 1)
                if back:
                    dve.wait_ge(oddH_ready, s + 1)
                    dve.tensor_tensor(oddL[:, :, :], c1[:, :, 1, :], oddH[:, :, :].bitcast(F32), ALU.subtract).then_inc(oddL_ready, 1)
                    dve.wait_ge(ms_full, 2 * s + 1)
                    dve.tensor_tensor(ms[:, 0:2, :], P_ms[0][:, 0:264].rearrange("p (j c) -> p j c", j=2),
                                      b_ms[:, :].unsqueeze(1).to_broadcast([128, 2, 132]), ALU.add).then_inc(ms_ready, 1)
                    dve.wait_ge(ms_full, 2 * s + 2)
                    dve.tensor_tensor(ms[:, 2:4, :], P_ms[1][:, 0:264].rearrange("p (j c) -> p j c", j=2),
                                      b_ms[:, :].unsqueeze(1).to_broadcast([128, 2, 132]), ALU.add).then_inc(ms_ready, 1)
                    dve.wait_ge(ms_ready, 2 * s + 2)
                    s_bc = ms[:, :, D:D + S3].unsqueeze(2).to_broadcast([128, 4, 2, S3])
                    vm = cb.mark(dve.tensor_copy(
                        feat[:, :, 0:6].rearrange("p t (a k) -> p t a k", a=2).bitcast(F32R), s_bc))
                    vq = cb.mark(dve.scalar_tensor_tensor(sq[:, :, :], ms[:, :, D:D + S3], -1.0, ms[:, :, D:D + S3],
                                                          ALU.mult, ALU.mult))
                    dve.wait_ge(cb.sem, vm)
                    dve.tensor_tensor(feat[:, :, 6:12].rearrange("p t (a k) -> p t a k", a=2), s_bc,
                                      feat[:, :, 0:6].rearrange("p t (a k) -> p t a k", a=2),
                                      ALU.subtract).then_inc(feat_split, 1)
                    dve.wait_ge(cb.sem, vq)
                    vq = cb.mark(dve.reduce_sum(nsq[:, :], sq[:, :, :], AX.X))
                    dve.wait_ge(cb.sem, vq)
                    both = feat[:, :, 12:80].rearrange("p t (a k) -> p t a k", a=2)
                    nsq_bc = nsq[:, :].unsqueeze(2).to_broadcast([128, 4, 2])
                    vm = cb.mark(dve.tensor_copy(both[:, :, :, 0].bitcast(F32R), nsq_bc))
                    dve.wait_ge(feat_right, s + 1)
                    dve.wait_ge(cb.sem, vm)
                    dve.tensor_tensor(both[:, :, :, 1], nsq_bc, both[:, :, :, 0], ALU.subtract).then_inc(feat_ready, 1)
                if mid:
                    cm.start(q)
                    dve.wait_ge(y_full, q + 1)
                    dve.tensor_tensor(y[:, :].rearrange("p (j f) -> p j f", j=4),
                                      P_y[:, :].rearrange("p (j f) -> p j f", j=4),
                                      rden[:, uq, :].unsqueeze(2).to_broadcast([128, 4, D]), ALU.mult).then_inc(y_ready, 1)
                if final:
                    ce.start(e)
                    dve.wait_ge(hmn_ready, e + 1)
                    dve.wait_ge(tz_ready, e + 1)
                    v = ce.mark(dve.scalar_tensor_tensor(zw[:, :], tz[:, :], 1.0, hmn[:, :], ALU.add, ALU.mult))
                    dve.wait_ge(ce.sem, v)
                    dve.scalar_tensor_tensor(og[:, :], zw[:, :], 0.5, ng[:, :], ALU.mult, ALU.add).then_inc(og_ready, 1)
                    ce.end()
                if mid:
                    dve.wait_ge(y_ready, q + 1)
                    v = cm.mark(dve.scalar_tensor_tensor(xsum[:, :, :], y[:, :].rearrange("p (j f) -> p j f", j=4), 0.0,
                                                         x_sb[:, uq], ALU.max, ALU.add))
                    dve.wait_ge(yexp_ready, q + 1)
                    v = cm.mark(dve.tensor_scalar(eneg[:, :, :], yexp[:, :].rearrange("p (j f) -> p j f", j=4), 1.0, -1.0,
                                                  ALU.min, ALU.add))
                if final:
                    dve.wait_ge(outT_full, e + 1)
                    if at is None or at >= 3:
                        dve.wait_ge(out_stored[ue], 16 * (half - 1 + u))
                    dve.tensor_tensor(x2[:, ue], P_outT[:, :].rearrange("p (j f) -> p j f", j=4), x1[:, ue],
                                      ALU.add).then_inc(x2_ready, 1)
                if back:
                    dve.wait_ge(aff_ready, 2 * s + 1)
                    dve.tensor_tensor(affm[:, 0, :, :], aff[:, 0, :, :], adjT[:, u, 0, :, :], ALU.mult).then_inc(affm_ready, 1)
                if mid:
                    if final:
                        dve.wait_ge(x2_ready, e + 1)
                    dve.wait_ge(cm.sem, v)
                    dve.tensor_tensor(x1[:, uq], xsum[:, :, :], eneg[:, :, :], ALU.add).then_inc(x1_ready, 1)
                if back:
                    dve.wait_ge(hTb_ready, s + 1)
                    dve.wait_ge(odd_full, s + 1)
                    dve.scalar_tensor_tensor(xcu[:, :].rearrange("p (n h) -> p n h", h=2),
                                             P_odd[:, 0:N].unsqueeze(2).to_broadcast([128, N, 2]), bnscale[:, 1:2],
                                             hTb[:, :].rearrange("p (n h) -> p n h", h=2),
                                             ALU.mult, ALU.add).then_inc(xcu_ready, 1)
                if mid:
                    dve.wait_ge(x1_ready, q + 1)
                    for j in range(4):
                        v = dve.bn_stats(st1[:, j, :], x1[:, uq, j, :])
                    v = cm.mark(v)
                if front:
                    dve.wait_ge(deg_ready, p + 1)
                    dve.tensor_scalar(some[:, 0, :], deg[:, :], 0.0, None, ALU.is_gt)
                if mid:
                    dve.wait_ge(cm.sem, v)
                if front:
                    vs = cf.mark(dve.tensor_scalar(some[:, 1, :], deg[:, :], float(N), None, ALU.is_ge))
                if mid:
                    for j in range(4):
                        v = dve.bn_aggr(mv1[:, j, :], st1[:, j, :])
                    v = cm.mark(v)
                if front:
                    dve.wait_ge(cf.sem, vs)
                    cf.mark(dve.tensor_scalar(fill[:, :, :], some[:, :, :], -1.0, -NEG, ALU.add, ALU.mult))
                if at == FIRST_STEP:
                    prepare_vectors()
                if mid:
                    dve.wait_ge(cm.sem, v)
                    v = cm.mark(dve.tensor_scalar(var1[:, :], mv1[:, :, 1], EPS, None, ALU.add))
                    cm.mark(dve.tensor_tensor(g1[:, :, :], x1[:, uq], mv1[:, :, 0].unsqueeze(2).to_broadcast([128, 4, D]),
                                              ALU.subtract))
                    dve.wait_ge(cm.sem, v)
                    v = cm.mark(dve.tensor_scalar(seed1[:, :].bitcast(I32), var1[:, :].bitcast(I32), -0.5, RSQRT_SEED,
                                                  ALU.mult, ALU.add))
                if front:
                    dve.wait_ge(sprod_ready, p + 1)
                    vf = cf.mark(dve.reduce_sum(srow[:, :], sprod[:, :, :], AX.X))
                for it in range(3):
                    if it == 2 and back:
                        dve.wait_ge(nmpH_ready, s + 1)
                        dve.tensor_tensor(nmpL[:, :], P_nmp[:, :], nmpH[:, :].bitcast(F32), ALU.subtract).then_inc(nmpL_ready, 1)
                    old, new = (seed1, yb1, seed1)[it], (yb1, seed1, rstd1)[it]
                    if mid:
                        dve.wait_ge(cm.sem, v)
                        v = cm.mark(dve.scalar_tensor_tensor(ya1[:, :], old[:, :], -0.5, old[:, :], ALU.mult, ALU.mult))
                    if front:
                        dve.wait_ge(cf.sem, vf)
                        if it == 0:
                            vf = cf.mark(dve.scalar_tensor_tensor(erow[:, :], srow[:, :], ALPHA, srow[:, :],
                                                                  ALU.mult, ALU.max))
                        elif it == 1:
                            vf = cf.mark(dve.tensor_tensor(cand[:, :, :], cand[:, :, :], fill[:, :, :], ALU.add))
                        else:
                            dve.tensor_tensor(sraw[:, 0, :], erow[:, :], rmax[:, :], ALU.subtract)
                            vf = cf.mark(dve.tensor_scalar(sraw[:, 1, :], rmax[:, :], -1.0, NEG, ALU.mult, ALU.add))
                    if mid:
                        dve.wait_ge(cm.sem, v)
                        v = cm.mark(dve.tensor_tensor(ya1[:, :], ya1[:, :], var1[:, :], ALU.mult))
                    if front:
                        dve.wait_ge(cf.sem, vf)
                        if it == 0:
                            vf = cf.mark(dve.tensor_tensor(cand[:, :, :], some[:, :, :],
                                                           erow[:, :].unsqueeze(1).to_broadcast([128, 2, 4]), ALU.mult))
                        elif it == 1:
                            vf = cf.mark(dve.tensor_tensor(rmax[:, :], cand[:, 0, :], cand[:, 1, :], ALU.max))
                        else:
                            dve.tensor_scalar(sdiff[:, :, :], sraw[:, :, :], 0.0, None, ALU.min).then_inc(sdiff_ready, 1)
                    if mid:
                        dve.wait_ge(cm.sem, v)
                        v = cm.mark(dve.scalar_tensor_tensor(new[:, :], ya1[:, :], 1.5, old[:, :], ALU.add, ALU.mult))
                if back:
                    dve.wait_ge(xcu_ready, s + 1)
                    dve.wait_ge(conv2_full, s + 1)
                    dve.scalar_tensor_tensor(xcp[:, :].rearrange("p (n h) -> p n h", h=2),
                                             P_conv2[:, :].rearrange("p (h n) -> p n h", h=2), bnscale[:, 1:2],
                                             xcu[:, :].rearrange("p (n h) -> p n h", h=2),
                                             ALU.mult, ALU.add).then_inc(xcp_ready, 1)
                if mid:
                    dve.wait_ge(cm.sem, v)
                    dve.scalar_tensor_tensor(h1[:, :, :], g1[:, :, :], 0.0,
                                             rstd1[:, :].unsqueeze(2).to_broadcast([128, 4, D]),
                                             ALU.max, ALU.mult).then_inc(h1_ready, 1)
                    cm.end()
                if at == PREP_STEP:
                    prepare_back(LAST_GROUPS)
                if back:
                    dve.wait_ge(xcH_ready, s + 1)
                    dve.scalar_tensor_tensor(xcL[:, :], xcp[:, :], 0.0, xcH[:, :].bitcast(F32),
                                             ALU.max, ALU.subtract).then_inc(xcL_ready, 1)
                if front:
                    dve.wait_ge(dsum_ready, p + 1)
                    vd = cf.mark(dve.scalar_tensor_tensor(den[:, :], pexp[:, 1, :], float(N), dsum[:, :], ALU.mult, ALU.add))
                    dve.wait_ge(cf.sem, vd)
                    dve.reciprocal(rden[:, up, :], den[:, :])
                    cf.end()
                if back:
                    dve.wait_ge(nh_ready, s + 1)
                    dve.wait_ge(tr_ready, s + 1)
                    dve.scalar_tensor_tensor(rn[:, :], tr[:, :], 1.0, nh[:, :], ALU.add, ALU.mult).then_inc(rn_ready, 1)
                    cb.end()

            steps(dve, step, prepare, loop_from=LOOP_FROM + 2)


NAMES = ["x", "adj", "L0_gnn_W", "L0_gnn_a", "L1_gnn_w_se", "L1_gnn_b_se", "L1_gnn_conv1_w", "L1_gnn_bn1_g",
         "L1_gnn_bn1_b", "L1_gnn_bn1_m", "L1_gnn_bn1_v", "L1_gnn_conv2_w", "L1_gnn_bn2_g", "L1_gnn_bn2_b",
         "L1_gnn_bn2_m", "L1_gnn_bn2_v", "L1_gnn_w_msg", "L1_gnn_b_msg", "L1_gnn_w_ih", "L1_gnn_b_ih",
         "L1_gnn_w_hh", "L1_gnn_b_hh"]


def kernel(**inputs):
    import concourse.bacc as bacc
    from concourse.bass_utils import run_bass_kernel_spmd

    nc = bacc.Bacc("TRN2", target_bir_lowering=False, num_devices=1)
    arrays, args = {}, []
    for name in NAMES:
        v = np.ascontiguousarray(inputs[name])
        arrays[f"in_{name}"] = v
        args.append(nc.dram_tensor(f"in_{name}", v.shape, mybir.dt.from_np(v.dtype), kind="ExternalInput").ap())
    args.append(nc.dram_tensor("out_x", (B, N, D), F32, kind="ExternalOutput").ap())
    bass_gnn_kernel(nc, *args)
    result = run_bass_kernel_spmd(nc, [arrays], core_ids=[0])
    return result.results[0]["out_x"]
```
